# Optimizing a Trainium2 kernel written in Bass

```python
import numpy as np
import jax
import jax.numpy as jnp

def _softmax(x, axis=-1):
    return jax.nn.softmax(x, axis=axis)

def _gelu(x):
    return jax.nn.gelu(x, approximate=True)

def _silu(x):
    return jax.nn.silu(x)

def _sigmoid(x):
    return jax.nn.sigmoid(x)

def _layernorm(x, axis=-1, eps=1e-05):
    m = jnp.mean(x, axis=axis, keepdims=True)
    v = jnp.var(x, axis=axis, keepdims=True)
    return (x - m) / jnp.sqrt(v + eps)

def _scatter_add(tgt, idx, src, axis=0):
    return tgt.at[idx].add(src)

def _segment_sum(src, seg, n):
    return jax.ops.segment_sum(src, seg, n)
kernel_name = 'mk_adaln_d1_jaxref_r8_c50efc'

def setup_inputs(seed: int=0):
    np.random.seed(seed)
    _w = jnp.asarray

    def _L0_attn_setup():
        import jax, jax.numpy as jnp
        import numpy as np
        import math
        B, S, E = (2, 256, 128)
        H, DK, DV = (16, 64, 64)

        def _rope(q, k):
            D = q.shape[-1]
            theta = 10000.0 ** (jnp.arange(0, D, 2, dtype=jnp.float32) / D)
            pos = jnp.arange(q.shape[-2], dtype=jnp.float32)
            freqs = pos[:, None] * (1.0 / theta)[None, :]
            emb = jnp.concatenate([freqs, freqs], axis=-1)
            cos = jnp.cos(emb)[None, None]
            sin = jnp.sin(emb)[None, None]

            def rotate(x):
                x1 = x[..., ::2]
                x2 = x[..., 1::2]
                return jnp.stack([-x2, x1], axis=-1).reshape(x.shape)
            return (q * cos + rotate(q) * sin, k * cos + rotate(k) * sin)
        key = jax.random.key(seed)
        ks = jax.random.split(key, 9)
        sE = 1.0 / math.sqrt(E)
        sV = 1.0 / math.sqrt(H * DV)
        return {'x': jax.random.normal(ks[0], (B, S, E), dtype=jnp.float32), 'wq': jax.random.uniform(ks[1], (H * DK, E), jnp.float32, -sE, sE), 'bq': jax.random.uniform(ks[2], (H * DK,), jnp.float32, -sE, sE), 'wk': jax.random.uniform(ks[3], (H * DK, E), jnp.float32, -sE, sE), 'bk': jax.random.uniform(ks[4], (H * DK,), jnp.float32, -sE, sE), 'wv': jax.random.uniform(ks[5], (H * DV, E), jnp.float32, -sE, sE), 'bv': jax.random.uniform(ks[6], (H * DV,), jnp.float32, -sE, sE), 'wo': jax.random.uniform(ks[7], (E, H * DV), jnp.float32, -sV, sV), 'bo': jax.random.uniform(ks[8], (E,), jnp.float32, -sV, sV)}
    _L0_attn_in = _L0_attn_setup()

    def _L0_ffn_setup():
        import jax, jax.numpy as jnp
        import numpy as np
        B, L, D = (4, 64, 128)
        E, TOP_K = (16, 4)
        F = 4 * D
        key = jax.random.key(seed)
        ks = jax.random.split(key, 6)
        scale = 0.02
        return {'x': jax.random.normal(ks[0], (B, L, D), jnp.float32), 'keys': jax.random.normal(ks[1], (E, D), jnp.float32), 'w1': jax.random.normal(ks[2], (E, F, D), jnp.float32) * scale, 'b1': jnp.zeros((E, F), jnp.float32), 'w2': jax.random.normal(ks[3], (E, D, F), jnp.float32) * scale, 'b2': jnp.zeros((E, D), jnp.float32), 'rw': jax.random.normal(ks[4], (E, D), jnp.float32) * scale, 'rb': jnp.zeros((E,), jnp.float32)}
    _L0_ffn_in = _L0_ffn_setup()
    _L0_c = _w((lambda *s: np.random.randn(*s).astype(np.float32) * 0.05)(4, 128))
    _L0_wmod = _w((lambda *s: np.random.randn(*s).astype(np.float32) * 0.05)(128, 6 * 128) * 128 ** (-0.5))
    _d = {'L0_attn_x': _L0_attn_in['x'], 'L0_attn_wq': _L0_attn_in['wq'], 'L0_attn_bq': _L0_attn_in['bq'], 'L0_attn_wk': _L0_attn_in['wk'], 'L0_attn_bk': _L0_attn_in['bk'], 'L0_attn_wv': _L0_attn_in['wv'], 'L0_attn_bv': _L0_attn_in['bv'], 'L0_attn_wo': _L0_attn_in['wo'], 'L0_attn_bo': _L0_attn_in['bo'], 'L0_ffn_keys': _L0_ffn_in['keys'], 'L0_ffn_w1': _L0_ffn_in['w1'], 'L0_ffn_b1': _L0_ffn_in['b1'], 'L0_ffn_w2': _L0_ffn_in['w2'], 'L0_ffn_b2': _L0_ffn_in['b2'], 'L0_ffn_rw': _L0_ffn_in['rw'], 'L0_ffn_rb': _L0_ffn_in['rb'], 'L0_c': _L0_c, 'L0_wmod': _L0_wmod}
    _x0 = _d['L0_attn_x']
    _d['L0_attn_x'] = jax.random.normal(jax.random.fold_in(jax.random.key(seed), 1), (4, 512, 128), dtype=_x0.dtype)
    del _x0
    return _d

def reference(L0_attn_x, L0_attn_wq, L0_attn_bq, L0_attn_wk, L0_attn_bk, L0_attn_wv, L0_attn_bv, L0_attn_wo, L0_attn_bo, L0_ffn_keys, L0_ffn_w1, L0_ffn_b1, L0_ffn_w2, L0_ffn_b2, L0_ffn_rw, L0_ffn_rb, L0_c, L0_wmod):

    def _L0_attn_ref(x, wq, bq, wk, bk, wv, bv, wo, bo):
        import jax, jax.numpy as jnp
        import numpy as np
        import math
        B, S, E = (2, 256, 128)
        H, DK, DV = (16, 64, 64)

        def _rope(q, k):
            D = q.shape[-1]
            theta = 10000.0 ** (jnp.arange(0, D, 2, dtype=jnp.float32) / D)
            pos = jnp.arange(q.shape[-2], dtype=jnp.float32)
            freqs = pos[:, None] * (1.0 / theta)[None, :]
            emb = jnp.concatenate([freqs, freqs], axis=-1)
            cos = jnp.cos(emb)[None, None]
            sin = jnp.sin(emb)[None, None]

            def rotate(x):
                x1 = x[..., ::2]
                x2 = x[..., 1::2]
                return jnp.stack([-x2, x1], axis=-1).reshape(x.shape)
            return (q * cos + rotate(q) * sin, k * cos + rotate(k) * sin)
        Bx, Sx, Ex = x.shape
        q = (x @ wq.T + bq).reshape(Bx, Sx, H, DK).transpose(0, 2, 1, 3)
        k = (x @ wk.T + bk).reshape(Bx, Sx, H, DK).transpose(0, 2, 1, 3)
        v = (x @ wv.T + bv).reshape(Bx, Sx, H, DV).transpose(0, 2, 1, 3)
        q, k = _rope(q, k)
        scores = jnp.einsum('bhqd,bhkd->bhqk', q, k)
        causal = jnp.triu(jnp.ones((Sx, Sx), dtype=bool), k=1)
        scores = jnp.where(causal[None, None], -jnp.inf, scores)
        attn = jax.nn.softmax(scores / math.sqrt(DK), axis=-1)
        out = jnp.einsum('bhqk,bhkd->bhqd', attn, v)
        out = out.transpose(0, 2, 1, 3).reshape(Bx, Sx, H * DV)
        return out @ wo.T + bo

    def _L0_ffn_ref(x, keys, w1, b1, w2, b2, rw, rb):
        import jax, jax.numpy as jnp
        import numpy as np
        B, L, D = (4, 64, 128)
        E, TOP_K = (16, 4)
        F = 4 * D
        diff = x[:, :, None, :] - keys
        dist2 = jnp.sum(diff * diff, axis=-1)
        logits = -dist2 + jnp.einsum('bld,ed->ble', x, rw) + rb
        topv, topi = jax.lax.top_k(logits, TOP_K)
        w = jax.nn.softmax(topv, axis=-1)
        hidden = jax.nn.gelu(jnp.einsum('bld,efd->blef', x, w1) + b1, approximate=False)
        exp_out = jnp.einsum('blef,edf->bled', hidden, w2) + b2
        sel = jnp.take_along_axis(exp_out, topi[..., None], axis=2)
        fused = jnp.sum(w[..., None] * sel, axis=2)
        return fused
    x = L0_attn_x
    mod = (_silu(L0_c) @ L0_wmod).reshape(L0_c.shape[0], 6, 1, -1)
    sa, ca, ga, sb, cb, gb = (mod[:, 0], mod[:, 1], mod[:, 2], mod[:, 3], mod[:, 4], mod[:, 5])
    ga = (2 * (ga >= 0) - 1) * jnp.maximum(jnp.abs(ga), 0.25)
    gb = (2 * (gb >= 0) - 1) * jnp.maximum(jnp.abs(gb), 0.25)
    h = _layernorm(x, axis=-1) * (1 + ca) + sa
    x = x + ga * _L0_attn_ref(h, L0_attn_wq, L0_attn_bq, L0_attn_wk, L0_attn_bk, L0_attn_wv, L0_attn_bv, L0_attn_wo, L0_attn_bo)
    h = _layernorm(x, axis=-1) * (1 + cb) + sb
    x = x + gb * _L0_ffn_ref(h, L0_ffn_keys, L0_ffn_w1, L0_ffn_b1, L0_ffn_w2, L0_ffn_b2, L0_ffn_rw, L0_ffn_rb)
    return x

_drawn_inputs = setup_inputs


def setup_inputs(seed=0):
    import zlib

    import numpy as np

    out = dict(_drawn_inputs(seed))
    spreads = {'L0_ffn_b1': (0.0, 0.8), 'L0_ffn_b2': (0.0, 0.331), 'L0_ffn_rb': (0.0, 2.0)}
    factors = {'L0_attn_wq': 8.0,
     'L0_attn_bq': 8.0,
     'L0_attn_wk': 8.0,
     'L0_attn_bk': 8.0,
     'L0_attn_wv': 5.706,
     'L0_attn_bv': 7.245,
     'L0_attn_wo': 4.677,
     'L0_attn_bo': 25.275,
     'L0_ffn_w1': 4.405,
     'L0_ffn_w2': 3.966,
     'L0_ffn_rw': 8.0}
    for name, (base, spread) in spreads.items():
        noise = np.random.default_rng([zlib.crc32(name.encode()), seed]).standard_normal(out[name].shape)
        drawn = base * np.exp(spread * noise) if base else spread * noise
        out[name] = jnp.asarray(drawn.astype(out[name].dtype))
    for name, factor in factors.items():
        out[name] = (out[name] * factor).astype(out[name].dtype)
    return out
```

```python
import concourse.bass as bass
from concourse import mybir
from contextlib import ExitStack

B, S, E = 4, 512, 128
H, DH = 16, 64
HP = H * DH // 128
TOK = B * S
NT = TOK // 128
QT = S // 128
NX, F, TOPK = 16, 512, 4
FT = F // 128
UNITS = HP * B
WS = 16.0
SCORE_SCALE = DH ** -0.5
EPS = 1e-5
NEG = -1.0e30
FAR = 3.0e38


def adaln_block(nc, x, c_t, wmod, w_qkv, b_qk, bv_rows, wo_t, bo_rows, keys_t, rw_t, rb_row, w1_t, b1_t, w2_t, b2,
                cos_sin, causal, identity, out):
    f32, f16 = mybir.dt.float32, mybir.dt.float16
    ALU = mybir.AluOpType
    ACT = mybir.ActivationFunctionType
    AX = mybir.AxisListType
    ds = bass.ds

    with ExitStack() as ctx:
        def sb(name, shape, dt=f32):
            return ctx.enter_context(nc.sbuf_tensor(name, shape, dt))

        def sem(name):
            return ctx.enter_context(nc.semaphore(name))

        x_tok = sb("x_tok", [128, NT, E])
        big = sb("big", [128, UNITS * S])
        vo = big[:, :].rearrange("p (g b i d) -> p g b i d", g=HP, b=B, i=QT)
        w_raw = big[:, 0:5 * 1024]
        wo_raw = big[:, 5 * 1024:6 * 1024]
        xn = big[:, UNITS * S - NT * E:UNITS * S].rearrange("p (t e) -> p t e", t=NT)
        h_f32 = sb("h_f32", [128, TOK])
        h_hi = sb("h_hi", [128, TOK], f16)
        h_lo = sb("h_lo", [128, TOK], f16)
        w_hi = sb("w_hi", [128, 5, 1024], f16)
        w_lo = sb("w_lo", [128, 5, 1024], f16)
        wo_hi = sb("wo_hi", [128, HP, E], f16)
        wo_lo = sb("wo_lo", [128, HP, E], f16)
        ident = sb("ident", [128, 128])
        mask = sb("mask", [128, S])
        rope = sb("rope", [128, 2, S])
        bqk = sb("bqk", [128, 4, HP])
        bv_b = sb("bv_b", [128, 1024])
        bo_b = sb("bo_b", [128, E])
        c_col = sb("c_col", [128, B])
        c_tmp = sb("c_tmp", [128, B])
        silu_c = sb("silu_c", [128, B])
        silu_b = sb("silu_b", [128, B, 128])
        wm = sb("wm", [128, 6, 128])
        mod_t = sb("mod_t", [128, 4, B])
        gate_a = sb("gate_a", [128, B, E])
        gate_b = sb("gate_b", [128, B, E])
        sign_t = sb("sign_t", [128, B, E])
        stats = sb("stats", [128, NT, 6])
        mv = sb("mv", [128, NT, 2])
        var_e = sb("var_e", [128, NT])
        rstd = sb("rstd", [128, NT])
        half = sb("half", [128, NT])
        rot_c = [sb(f"rot_c{m}", [128, S]) for m in range(2)]
        rot_s = [sb(f"rot_s{m}", [128, S]) for m in range(2)]
        rot = [sb(f"rot{m}", [128, S]) for m in range(2)]
        qk_hi = [[sb(f"qk_hi{m}{v}", [128, S], f16) for v in range(2)] for m in range(2)]
        qk_lo = [[sb(f"qk_lo{m}{v}", [128, S], f16) for v in range(2)] for m in range(2)]
        p_sb = [[sb(f"p_sb{s}{a}", [128, S]) for a in range(2)] for s in range(2)]
        pt_sb = [[sb(f"pt_sb{s}{a}", [128, S]) for a in range(2)] for s in range(2)]
        row_max = [sb(f"row_max{v}", [128, 2 * QT]) for v in range(2)]
        row_sum = [sb(f"row_sum{v}", [128, 2 * QT]) for v in range(2)]
        row_inv = sb("row_inv", [128, QT, 2])
        waited = sb("waited", [128, QT])
        ot = sb("ot", [128, HP * S])
        ot_hi = ot[:, 0:HP * S // 2].bitcast(f16).rearrange("p (g s) -> p g s", g=HP)
        ot_lo = ot[:, HP * S // 2:HP * S].bitcast(f16).rearrange("p (g s) -> p g s", g=HP)
        o_mid = [sb(f"o_mid{v}", [128, S]) for v in range(2)]
        h_sq = rot_c[0]
        k_t = sb("k_t", [128, NX])
        k_w = sb("k_w", [128, NX])
        rw_sb = sb("rw_sb", [128, NX])
        k_neg = sb("k_neg", [128, NX])
        ones = sb("ones", [128, 128])
        minus = sb("minus", [128, NX])
        rb_sb = sb("rb_sb", [1, NX])
        logit = sb("logit", [128, NT, NX + 4])
        taken = sb("taken", [128, NT, NX + 4])
        top = sb("top", [128, NT, 8])
        gates = sb("gates", [128, NT, NX])
        gsum = sb("gsum", [128, NT])
        gates_t = sb("gates_t", [NX, TOK])
        b2_sb = sb("b2_sb", [NX, E])
        b1_sb = sb("b1_sb", [128, NX, FT])
        b1_now = [sb(f"b1_now{w}", [128, FT]) for w in range(2)]
        ws_col = sb("ws_col", [128, 1])
        acc = ot[:, 0:NT * E].rearrange("p (t e) -> p t e", t=NT)

        at = [0]

        def carve(cols, dt=f32):
            words = cols if dt == f32 else cols // 2
            ap = big[:, at[0]:at[0] + words]
            at[0] += words
            return ap if dt == f32 else ap.bitcast(dt)

        g_f32 = [[carve(S) for _ in range(FT)] for _ in range(2)]
        g_hi = [[carve(S, f16) for _ in range(FT)] for _ in range(2)]
        g_lo = [[carve(S, f16) for _ in range(FT)] for _ in range(2)]
        wx_raw = [carve(2 * F) for _ in range(2)]
        wx_f32 = carve(2 * F)
        wx_hi = [carve(2 * F, f16) for _ in range(2)]
        wx_lo = [carve(2 * F, f16) for _ in range(2)]
        weighted = [carve(S) for _ in range(2)]
        assert at[0] <= UNITS * S - NT * E

        bank = [ctx.enter_context(nc.psum_tensor(f"bank{n}", [128, 512], f32)) for n in range(8)]

        ld_x, ld_c, ld_w, ld_k, ld_b = sem("ld_x"), sem("ld_c"), sem("ld_w"), sem("ld_k"), sem("ld_b")
        consts, silu_e, silu_v, mod_mm, mod_ev = sem("consts"), sem("silu_e"), sem("silu_v"), sem("mod_mm"), sem("mod_ev")
        split_hi, split_lo = sem("split_hi"), sem("split_lo")
        dve_own = sem("dve_own")
        ln_var, ln_rstd, ln_xn, ln_tr, ln_f32, ln_hi, ln_lo = (sem(n) for n in (
            "ln_var", "ln_rstd", "ln_xn", "ln_tr", "ln_f32", "ln_hi", "ln_lo"))
        v_mm, v_ev = sem("v_mm"), sem("v_ev")
        proj_mm, rot_parts, rot_sum, qk_hi_done, qk_lo_done = (sem(n) for n in (
            "proj_mm", "rot_parts", "rot_sum", "qk_hi_done", "qk_lo_done"))
        score_mm, masked, exp_done, pt_mm, pt_a, pt_b, pv_mm, o_ev = (sem(n) for n in (
            "score_mm", "masked", "exp_done", "pt_mm", "pt_a", "pt_b", "pv_mm", "o_ev"))
        ot_mm, ot_h, ot_l, wo_mm, wo_ev = (sem(n) for n in ("ot_mm", "ot_h", "ot_l", "wo_mm", "wo_ev"))
        sq_done, kw_done, logit_mm, logit_ev, shifted, gexp, gates_done, gt_mm, gt_ev, b2_mm, acc_set = (
            sem(n) for n in ("sq_done", "kw_done", "logit_mm", "logit_ev", "shifted", "gexp", "gates_done",
                             "gt_mm", "gt_ev", "b2_mm", "acc_set"))
        wx_ld = [sem("wx_ld0"), sem("wx_ld1")]
        wx_split, wx_own = sem("wx_split"), sem("wx_own")
        up_mm, gelu_done, g_hi_a, g_split, down_mm, weigh, acc_add = (sem(n) for n in (
            "up_mm", "gelu_done", "g_hi_a", "g_split", "down_mm", "weigh", "acc_add"))
        wx_hi_done, b1_here = sem("wx_hi_done"), sem("b1_here")
        o_ev_inv, kw_own, g_hi_v = sem("o_ev_inv"), sem("kw_own"), sem("g_hi_v")
        fin, stored = sem("fin"), sem("stored")

        block = ctx.enter_context(nc.Block())

        @block.sync
        def _(sp):
            sp.dma_start(x_tok[:, :, :], x.rearrange("(t p) e -> p t e", p=128)).then_inc(ld_x, 16)
            sp.dma_start(ident[:, :], identity).then_inc(ld_c, 16)
            sp.dma_start(c_col[:, :], c_t).then_inc(ld_c, 16)
            sp.dma_start(wm[:, :, :], wmod.rearrange("p (m e) -> p m e", m=6)).then_inc(ld_c, 16)
            sp.dma_start(w_raw, w_qkv).then_inc(ld_w, 16)
            sp.dma_start(wo_raw, wo_t).then_inc(ld_w, 16)
            sp.dma_start(bv_b[:, :], bv_rows).then_inc(ld_b, 16)
            sp.dma_start(rope[:, :, :], cos_sin).then_inc(ld_b, 16)
            sp.dma_start(bqk[:, :, :], b_qk).then_inc(ld_b, 16)
            sp.dma_start(mask[:, :], causal).then_inc(ld_b, 16)
            sp.dma_start(bo_b[:, :], bo_rows).then_inc(ld_b, 16)
            sp.dma_start(k_t[:, :], keys_t).then_inc(ld_k, 16)
            sp.dma_start(rw_sb[:, :], rw_t).then_inc(ld_k, 16)
            sp.dma_start(rb_sb[:, :], rb_row).then_inc(ld_k, 16)
            sp.dma_start(b2_sb[:, :], b2).then_inc(ld_k, 16)
            sp.dma_start(b1_sb[:, :, :], b1_t).then_inc(ld_k, 16)
            sp.wait_ge(ot_mm, B * HP)
            for e in range(2):
                sp.dma_start(wx_raw[e][:, 0:F], w1_t[e, :, :]).then_inc(wx_ld[e], 16)
                sp.dma_start(wx_raw[e][:, F:2 * F], w2_t[e, :, :]).then_inc(wx_ld[e], 16)
            with sp.Fori(1, NX // 2) as pair:
                for e in range(2):
                    sp.wait_ge(wx_split, pair * 2 + (e - 1))
                    sp.dma_start(wx_raw[e][:, 0:F], w1_t[ds(pair * 2 + e, 1), :, :].squeeze(0)).then_inc(wx_ld[e], 16)
                    sp.dma_start(wx_raw[e][:, F:2 * F], w2_t[ds(pair * 2 + e, 1), :, :].squeeze(0)).then_inc(wx_ld[e], 16)
            for b in range(B):
                sp.wait_ge(fin, b + 1)
                sp.dma_start(out[b * S:(b + 1) * S, :].rearrange("(t p) e -> p t e", p=128),
                             acc[:, b * QT:(b + 1) * QT, :]).then_inc(stored, 16)
            sp.wait_ge(stored, 16 * B)

        @block.tensor
        def _(pe):
            mm = nc.tensor.matmul

            def three(dst, a_hi, a_lo, b_hi, b_lo, first=True, last=True):
                mm(dst, a_hi, b_hi, start=first, stop=False)
                mm(dst, a_hi, b_lo, start=False, stop=False)
                return mm(dst, a_lo, b_hi, start=False, stop=last)

            pe.wait_ge(ld_c, 48)
            pe.wait_ge(silu_v, 1)
            for n, m in enumerate((0, 1, 3, 4)):
                last = mm(bank[0][:, n * B:(n + 1) * B], wm[:, m, :], silu_c[:, :], start=True, stop=True)
            last.then_inc(mod_mm, 1)
            for n, m in enumerate((2, 5)):
                for b in range(B):
                    last = mm(bank[1 + n][:, b * E:(b + 1) * E], silu_b[:, b, :], wm[:, m, :], start=True, stop=True)
                last.then_inc(mod_mm, 1)

            def ln_transposes(ln):
                for b in range(B):
                    pe.wait_ge(ln_xn, ln * B + b + 1)
                    for i in range(QT):
                        last = nc.tensor.transpose(bank[4 + b][:, i * 128:(i + 1) * 128], xn[:, b * QT + i, :], ident[:, :])
                    last.then_inc(ln_tr, 1)

            ln_transposes(0)

            pe.wait_ge(ln_lo, B)
            pe.wait_ge(split_lo, 5)
            with pe.Fori(0, NT) as t:
                for half_ in range(2):
                    pe.wait_ge(v_ev, t * 2 + half_)
                    rows = ds(t * 128, 128)
                    cols = slice(half_ * 512, half_ * 512 + 512)
                    three(bank[half_][:, :], h_hi[:, rows], h_lo[:, rows], w_hi[:, 4, cols], w_lo[:, 4, cols]).then_inc(v_mm, 1)

            def project(hp, b, m):
                u = hp * B + b
                if m > 0 or not (isinstance(u, int) and u == 0):
                    pe.wait_ge(rot_parts, u * 4 + m)
                toks = slice(b * S, (b + 1) * S)
                cols = ds(hp * 128, 128)
                three(bank[0][:, :], w_hi[:, m, cols], w_lo[:, m, cols], h_hi[:, toks], h_lo[:, toks]).then_inc(proj_mm, 1)

            def scores(hp, b, i):
                u = hp * B + b
                v = b % 2
                if i == 0:
                    pe.wait_ge(qk_lo_done, u * 2 + 2)
                if i >= 2 or not (isinstance(u, int) and u == 0):
                    pe.wait_ge(masked, u * 8 + 2 * i - 2)
                n = (i + 1) * 128
                parts = ((qk_hi, qk_hi), (qk_hi, qk_lo), (qk_lo, qk_hi))
                for k, (q_part, k_part) in enumerate(parts):
                    for a in range(2):
                        rows = slice(a * 64, a * 64 + 64)
                        last = mm(bank[4 + (i % 2) * 2 + a][:, 0:n], q_part[0][v][rows, i * 128:(i + 1) * 128],
                                  k_part[1][v][rows, 0:n], start=k == 0, stop=k == 2)
                        if k == 2:
                            last.then_inc(score_mm, 1)

            def transposes(hp, b, i):
                u = hp * B + b
                g = u * QT + i
                for a in range(2):
                    pe.wait_ge(exp_done, g * 2 + (a + 1))
                    if i > 0 or not (isinstance(u, int) and u == 0):
                        pe.wait_ge((pt_a, pt_b)[a], g)
                    for j in range(i + 1):
                        last = nc.tensor.transpose(bank[2 + a][:, j * 128:(j + 1) * 128],
                                                   p_sb[i % 2][a][:, j * 128:(j + 1) * 128], ident[:, :])
                    last.then_inc(pt_mm, 1)

            def values(hp, b, i):
                u = hp * B + b
                g = u * QT + i
                pe.wait_ge(pt_a, g + 1)
                pe.wait_ge(pt_b, g + 1)
                if i == 0 and not (isinstance(u, int) and u == 0):
                    pe.wait_ge(o_ev, u)
                for a in range(2):
                    for j in range(i + 1):
                        last = mm(bank[1][:, i * 128 + a * 64:i * 128 + a * 64 + 64],
                                  pt_sb[i % 2][a][:, j * 128:(j + 1) * 128],
                                  big[:, ds(hp * (B * S) + b * S + j * 128 + a * 64, 64)],
                                  start=j == 0, stop=j == i)
                last.then_inc(pv_mm, 1)

            def before(hp, b, i, back):
                g = (b * QT + i) - back
                return (hp, g // QT, g % QT) if g >= 0 else (hp - 1, B + g // QT, g % QT)

            def group(hp, first=False, final=False):
                for b in range(B):
                    for i in range(QT):
                        scores(hp, b, i)
                        nxt = (hp, b + 1) if b + 1 < B else (hp + 1, 0)
                        more = i < 2 and not (final and b == B - 1)
                        if more:
                            project(*nxt, 2 * i)
                        if not (first and b == 0 and i < 1):
                            transposes(*before(hp, b, i, 1))
                        if more:
                            project(*nxt, 2 * i + 1)
                        if not (first and b == 0 and i < 2):
                            values(*before(hp, b, i, 2))

            pe.wait_ge(v_ev, 2 * NT)
            for m in range(4):
                project(0, 0, m)
            group(0, first=True)
            with pe.Fori(1, HP - 1) as hp:
                group(hp)
            group(HP - 1, final=True)
            transposes(HP - 1, B - 1, QT - 1)
            values(HP - 1, B - 1, QT - 2)
            values(HP - 1, B - 1, QT - 1)

            pe.wait_ge(o_ev, UNITS)
            for b in range(B):
                for hp in range(HP):
                    n = b * HP + hp
                    if n >= 4:
                        pe.wait_ge(ot_l, n - 3)
                    for i in range(QT):
                        last = nc.tensor.transpose(bank[n % 4][:, i * 128:(i + 1) * 128], vo[:, hp, b, i, :], ident[:, :])
                    last.then_inc(ot_mm, 1)
                pe.wait_ge(ot_l, (b + 1) * HP)
                pe.wait_ge(ot_h, (b + 1) * HP)
                if b >= 2:
                    pe.wait_ge(wo_ev, b - 1)
                for i in range(QT):
                    toks = slice(i * 128, (i + 1) * 128)
                    for hp in range(HP):
                        last = three(bank[4 + b % 2][:, toks], ot_hi[:, hp, toks], ot_lo[:, hp, toks],
                                     wo_hi[:, hp, :], wo_lo[:, hp, :], first=hp == 0, last=hp == HP - 1)
                last.then_inc(wo_mm, 1)

            pe.wait_ge(wo_ev, B)
            ln_transposes(1)

            pe.wait_ge(kw_done, 1)
            for t in range(NT):
                if t % QT == 0:
                    pe.wait_ge(ln_f32, B + t // QT + 1)
                    pe.wait_ge(sq_done, t // QT + 1)
                dst = bank[0][:, t * NX:(t + 1) * NX]
                mm(dst, h_f32[:, t * 128:(t + 1) * 128], k_w[:, :], start=True, stop=False)
                mm(dst, (rot_c + rot_s)[t // QT][:, (t % QT) * 128:(t % QT + 1) * 128], minus[:, :], start=False, stop=False)
                mm(dst, ones[:, :], k_neg[:, :], start=False, stop=False)
                last = mm(dst, ones[0:1, :], rb_sb[0:1, :], start=False, stop=True)
            last.then_inc(logit_mm, 1)
            pe.wait_ge(gates_done, 1)
            for b in range(B):
                for i in range(QT):
                    last = nc.tensor.transpose(bank[1 + b][0:NX, i * 128:(i + 1) * 128], gates[:, b * QT + i, :], ident[:, :])
                last.then_inc(gt_mm, 1)
            for b in range(B):
                pe.wait_ge(gt_ev, b + 1)
                for i in range(QT):
                    t = b * QT + i
                    last = mm(bank[1 + b][:, i * 128:(i + 1) * 128], gates_t[:, t * 128:(t + 1) * 128], b2_sb[:, :],
                              start=True, stop=True)
                last.then_inc(b2_mm, 1)

            def up(e, w, tb):
                n = e * B + tb
                toks = slice(tb * S, (tb + 1) * S)
                if tb == 0:
                    pe.wait_ge(wx_split, e + 1)
                for f in range(FT):
                    if not (isinstance(n, int) and n == 0):
                        pe.wait_ge(gelu_done, n * FT + (f + 1 - FT))
                    cols = slice(f * 128, (f + 1) * 128)
                    three(bank[f][:, :], wx_hi[w][:, cols], wx_lo[w][:, cols], h_hi[:, toks], h_lo[:, toks]).then_inc(up_mm, 1)

            def down(e, w, tb):
                n = e * B + tb
                v = tb % 2
                pe.wait_ge(g_split, n * FT + FT)
                pe.wait_ge(g_hi_a, n * 2 + 2)
                if not (isinstance(n, int) and n < 2):
                    pe.wait_ge(weigh, n - 1)
                for i in range(QT):
                    toks = slice(i * 128, (i + 1) * 128)
                    for f in range(FT):
                        cols = slice(F + f * 128, F + (f + 1) * 128)
                        last = three(bank[4 + v][:, toks], g_hi[v][f][:, toks], g_lo[v][f][:, toks],
                                     wx_hi[w][:, cols], wx_lo[w][:, cols], first=f == 0, last=f == FT - 1)
                last.then_inc(down_mm, 1)

            def expert_pair(pair, first=False):
                for w in range(2):
                    for tb in range(B):
                        up(pair * 2 + w, w, tb)
                        if not (first and w == 0 and tb == 0):
                            if tb:
                                down(pair * 2 + w, w, tb - 1)
                            else:
                                down(pair * 2 + w - 1, 1 - w, B - 1)

            pe.wait_ge(acc_set, B)
            pe.wait_ge(ln_lo, 2 * B)
            expert_pair(0, first=True)
            with pe.Fori(1, NX // 2) as pair:
                expert_pair(pair)
            down(NX - 1, 1, B - 1)

        @block.scalar
        def _(act):
            act.wait_ge(ld_c, 48)
            nc.scalar.activation(c_tmp[:, :], c_col[:, :], ACT.Exp, scale=-1.0).then_inc(silu_e, 1)
            act.wait_ge(ld_w, 32)
            for m in range(5):
                nc.scalar.activation(w_hi[:, m, :], w_raw[:, m * 1024:(m + 1) * 1024], ACT.Copy, scale=WS).then_inc(split_hi, 1)
            nc.scalar.activation(wo_hi[:, :, :], wo_raw.rearrange("p (g e) -> p g e", g=HP), ACT.Copy, scale=WS).then_inc(split_hi, 1)

            def ln_split(ln):
                for b in range(B):
                    act.wait_ge(ln_f32, ln * B + b + 1)
                    toks = slice(b * S, (b + 1) * S)
                    nc.scalar.activation(h_hi[:, toks], h_f32[:, toks], ACT.Copy).then_inc(ln_hi, 1)

            ln_split(0)

            def qk_round(hp, b, m):
                act.wait_ge(rot_sum, (hp * B + b) * 2 + (m + 1))
                nc.scalar.activation(qk_hi[m][b % 2][:, :], rot[m][:, :], ACT.Copy).then_inc(qk_hi_done, 1)

            def exps(hp, b, i):
                n = (i + 1) * 128
                for a in range(2):
                    k = 2 * i + a
                    act.wait_ge(masked, (hp * B + b) * 8 + (k + 1))
                    nc.scalar.activation(p_sb[i % 2][a][:, 0:n], p_sb[i % 2][a][:, 0:n], ACT.Exp,
                                         bias=row_max[b % 2][:, k:k + 1], scale=-1.0,
                                         accum_out=row_sum[b % 2][:, k:k + 1]).then_inc(exp_done, 1)

            def evacuate(hp, b, i):
                act.wait_ge(pt_mm, ((hp * B + b) * QT + i) * 2 + 1)
                n = (i + 1) * 128
                nc.scalar.activation(pt_sb[i % 2][0][:, 0:n], bank[2][:, 0:n], ACT.Copy).then_inc(pt_a, 1)

            def group(hp, first=False, final=False):
                for b in range(B):
                    nxt = (hp, b + 1) if b + 1 < B else (hp + 1, 0)
                    for i in range(QT):
                        exps(hp, b, i)
                        if not (first and b == 0 and i == 0):
                            g = b * QT + i - 1
                            evacuate(*((hp, g // QT, g % QT) if g >= 0 else (hp - 1, B - 1, QT - 1)))
                        if i in (1, 2) and not (final and b == B - 1):
                            qk_round(*nxt, i - 1)

            qk_round(0, 0, 0)
            qk_round(0, 0, 1)
            group(0, first=True)
            with act.Fori(1, HP - 1) as hp:
                group(hp)
            group(HP - 1, final=True)
            evacuate(HP - 1, B - 1, QT - 1)

            for n in range(B * HP):
                act.wait_ge(ot_mm, n + 1)
                if n % HP == 0 and n:
                    act.wait_ge(wo_mm, n // HP)
                nc.scalar.activation(ot_hi[:, n % HP, :], bank[n % 4][:, :], ACT.Copy).then_inc(ot_h, 1)

            ln_split(1)
            for b in range(B):
                nc.scalar.activation((rot_c + rot_s)[b][:, :], h_f32[:, b * S:(b + 1) * S], ACT.Square).then_inc(sq_done, 1)
            act.wait_ge(shifted, 1)
            nc.scalar.activation(gates[:, :, :], gates[:, :, :], ACT.Exp).then_inc(gexp, 1)

            def round_weights(e, w):
                act.wait_ge(wx_ld[w], (e - w) * 16 + 32)
                if not (isinstance(e, int) and e < 2):
                    act.wait_ge(down_mm, e * B - B)
                nc.scalar.activation(wx_hi[w], wx_raw[w], ACT.Copy, scale=WS).then_inc(wx_hi_done, 1)

            def hidden(e, w, tb):
                n = e * B + tb
                v = tb % 2
                if tb == 0:
                    act.wait_ge(ld_k, 80)
                    nc.scalar.activation(b1_now[w][:, :], b1_sb[:, ds(e, 1), :].squeeze(1), ACT.Copy).then_inc(b1_here, 1)
                    act.wait_ge(b1_here, e + 1)
                for f in range(FT):
                    act.wait_ge(up_mm, n * FT + (f + 1))
                    if not (isinstance(n, int) and n < 2):
                        act.wait_ge(g_split, n * FT + (f + 1 - 2 * FT))
                    nc.scalar.activation(g_f32[v][f], bank[f][:, :], ACT.Gelu,
                                         bias=b1_now[w][:, f:f + 1], scale=1.0 / WS).then_inc(gelu_done, 1)
                for f in range(2):
                    act.wait_ge(gelu_done, n * FT + (f + 1))
                    if not (isinstance(n, int) and n < 2):
                        act.wait_ge(down_mm, n - 1)
                    nc.scalar.activation(g_hi[v][f], g_f32[v][f], ACT.Copy).then_inc(g_hi_a, 1)

            def expert_pair(pair, last=False):
                for w in range(2):
                    for tb in range(B):
                        hidden(pair * 2 + w, w, tb)
                        if tb == 0 and w == 0 and not (isinstance(pair, int) and pair == 0):
                            round_weights(pair * 2 + 1, 1)
                        if tb == 0 and w == 1 and not last:
                            round_weights(pair * 2 + 2, 0)

            round_weights(0, 0)
            round_weights(1, 1)
            expert_pair(0)
            with act.Fori(1, NX // 2 - 1) as pair:
                expert_pair(pair)
            expert_pair(NX // 2 - 1, last=True)

        @block.vector
        def _(dve):
            own = [0]

            def step(ins):
                own[0] += 1
                ins.then_inc(dve_own, 1)
                dve.wait_ge(dve_own, own[0])

            v = nc.vector
            v.memset(ones[:, :], 1.0).then_inc(consts, 1)
            v.memset(minus[:, :], -1.0).then_inc(consts, 1)
            v.memset(half[:, :], -0.5).then_inc(consts, 1)
            v.memset(ws_col[:, :], WS).then_inc(consts, 1)
            v.memset(logit[:, :, NX:NX + 4], -FAR).then_inc(consts, 1)
            dve.wait_ge(silu_e, 1)
            step(v.tensor_scalar_add(c_tmp[:, :], c_tmp[:, :], 1.0))
            step(v.reciprocal(c_tmp[:, :], c_tmp[:, :]))
            step(v.tensor_tensor(silu_c[:, :], c_col[:, :], c_tmp[:, :], ALU.mult))
            v.tensor_copy(silu_b[:, :, :], silu_c[:, :].unsqueeze(2).broadcast_to([128, B, 128])).then_inc(silu_v, 1)

            def ln_normalise(ln):
                with dve.Fori(0, NT) as t:
                    v.bn_stats(stats[:, ds(t, 1), :].squeeze(1), x_tok[:, ds(t, 1), :].squeeze(1)).then_inc(dve_own, 1)
                own[0] += NT
                dve.wait_ge(dve_own, own[0])
                for t in range(NT):
                    v.bn_aggr(mv[:, t, :], stats[:, t, :]).then_inc(dve_own, 1)
                own[0] += NT
                dve.wait_ge(dve_own, own[0])
                v.tensor_scalar_add(var_e[:, :], mv[:, :, 1], EPS).then_inc(ln_var, 1)
                dve.wait_ge(ln_rstd, ln + 1)
                for b in range(B):
                    for i in range(QT):
                        t = b * QT + i
                        last = v.tensor_scalar(xn[:, t, :], x_tok[:, t, :], mv[:, t, 0:1], rstd[:, t:t + 1],
                                               ALU.subtract, ALU.mult)
                    last.then_inc(ln_xn, 1)

            def ln_modulate(ln):
                for b in range(B):
                    dve.wait_ge(ln_tr, ln * B + b + 1)
                    toks = slice(b * S, (b + 1) * S)
                    v.tensor_scalar(h_f32[:, toks], bank[4 + b][:, :], mod_t[:, 2 * ln + 1, b:b + 1],
                                    mod_t[:, 2 * ln, b:b + 1], ALU.mult, ALU.add).then_inc(ln_f32, 1)
                for b in range(B):
                    dve.wait_ge(ln_hi, ln * B + b + 1)
                    toks = slice(b * S, (b + 1) * S)
                    v.tensor_tensor(h_lo[:, toks], h_f32[:, toks], h_hi[:, toks], ALU.subtract).then_inc(ln_lo, 1)

            dve.wait_ge(ld_x, 16)
            ln_normalise(0)
            dve.wait_ge(mod_mm, 1)
            v.tensor_copy(mod_t[:, :, :], bank[0][:, 0:4 * B].rearrange("p (m b) -> p m b", m=4)).then_inc(mod_ev, 1)
            dve.wait_ge(mod_ev, 1)
            v.tensor_scalar_add(mod_t[:, 1, :], mod_t[:, 1, :], 1.0).then_inc(mod_ev, 1)
            v.tensor_scalar_add(mod_t[:, 3, :], mod_t[:, 3, :], 1.0).then_inc(mod_ev, 1)
            dve.wait_ge(mod_ev, 3)
            ln_modulate(0)
            for n, gate in enumerate((gate_a, gate_b)):
                dve.wait_ge(mod_mm, n + 2)
                src = bank[1 + n][:, :].rearrange("p (b e) -> p b e", b=B)
                step(v.tensor_copy(gate[:, :, :], src))
                step(v.tensor_scalar(sign_t[:, :, :], gate[:, :, :], 0.0, 2.0, ALU.is_ge, ALU.mult))
                step(v.scalar_tensor_tensor(gate[:, :, :], gate[:, :, :], -1.0, gate[:, :, :], ALU.mult, ALU.max))
                step(v.tensor_scalar_max(gate[:, :, :], gate[:, :, :], 0.25))
                step(v.scalar_tensor_tensor(gate[:, :, :], sign_t[:, :, :], -1.0, gate[:, :, :], ALU.add, ALU.mult))
            for m in range(5):
                dve.wait_ge(split_hi, m + 1)
                v.scalar_tensor_tensor(w_lo[:, m, :], w_raw[:, m * 1024:(m + 1) * 1024], WS, w_hi[:, m, :],
                                       ALU.mult, ALU.subtract).then_inc(split_lo, 1)
            dve.wait_ge(split_hi, 6)
            v.scalar_tensor_tensor(wo_lo[:, :, :], wo_raw.rearrange("p (g e) -> p g e", g=HP), WS, wo_hi[:, :, :],
                                   ALU.mult, ALU.subtract).then_inc(split_lo, 1)
            dve.wait_ge(ld_b, 80)
            step(v.tensor_scalar(bqk[:, :, :], bqk[:, :, :], WS, None, ALU.mult))
            dve.wait_ge(split_lo, 6)
            dve.wait_ge(ln_xn, B)
            big_v = big[:, :].rearrange("p (g r) -> p g r", g=HP)
            with dve.Fori(0, NT) as t:
                for half_ in range(2):
                    dve.wait_ge(v_mm, t * 2 + (half_ + 1))
                    v.scalar_tensor_tensor(
                        big_v[:, half_ * 4:half_ * 4 + 4, ds(t * 128, 128)],
                        bank[half_][:, :].rearrange("p (g d) -> p g d", g=4), 1.0 / WS,
                        bv_b[:, half_ * 512:half_ * 512 + 512].rearrange("p (g d) -> p g d", g=4),
                        ALU.mult, ALU.add).then_inc(v_ev, 1)

            def rotate(hp, b, m):
                u = hp * B + b
                dve.wait_ge(proj_mm, u * 4 + (m + 1))
                if not (isinstance(u, int) and u == 0):
                    dve.wait_ge(rot_sum, u * 2 + (m // 2 - 1))
                dst = (rot_c, rot_s)[m % 2][m // 2]
                v.scalar_tensor_tensor(dst[:, :], bank[0][:, :], bqk[:, m, ds(hp, 1)], rope[:, m % 2, :],
                                       ALU.add, ALU.mult).then_inc(rot_parts, 1)

            def mask_and_max(hp, b, i):
                n = (i + 1) * 128
                dve.wait_ge(score_mm, (hp * B + b) * 8 + (2 * i + 2))
                v.memset(waited[:, i:i + 1], 0.0)
                for a in range(2):
                    k = 2 * i + a
                    v.tensor_tensor_reduce(out=p_sb[i % 2][a][:, 0:n], in0=bank[4 + (i % 2) * 2 + a][:, 0:n],
                                           in1=mask[:, S - n:S], scale=-SCORE_SCALE, scalar=FAR, op0=ALU.add,
                                           op1=ALU.min, accum_out=row_max[b % 2][:, k:k + 1]).then_inc(masked, 1)

            def evacuate(hp, b, i):
                dve.wait_ge(pt_mm, ((hp * B + b) * QT + i) * 2 + 2)
                n = (i + 1) * 128
                v.tensor_copy(pt_sb[i % 2][1][:, 0:n], bank[3][:, 0:n]).then_inc(pt_b, 1)

            def output(hp, b):
                u = hp * B + b
                dve.wait_ge(exp_done, u * 8 + 8)
                v.reciprocal(row_inv[:, :, :], row_sum[b % 2][:, :].rearrange("p (i a) -> p i a", a=2)).then_inc(o_ev_inv, 1)
                dve.wait_ge(o_ev_inv, u + 1)
                dve.wait_ge(pv_mm, u * 4 + 4)
                v.tensor_tensor(big[:, ds(hp * (B * S) + b * S, S)].rearrange("p (i a d) -> p i a d", i=QT, a=2),
                                bank[1][:, :].rearrange("p (i a d) -> p i a d", i=QT, a=2),
                                row_inv[:, :, :].unsqueeze(3).broadcast_to([128, QT, 2, DH]), ALU.mult).then_inc(o_ev, 1)

            def group(hp, first=False, final=False):
                for b in range(B):
                    nxt = (hp, b + 1) if b + 1 < B else (hp + 1, 0)
                    prev = (hp, b - 1) if b else (hp - 1, B - 1)
                    for i in range(QT):
                        more = i < 2 and not (final and b == B - 1)
                        mask_and_max(hp, b, i)
                        if more:
                            rotate(*nxt, 2 * i)
                        if not (first and b == 0 and i == 0):
                            evacuate(*((hp, b, i - 1) if i else (*prev, QT - 1)))
                        if more:
                            rotate(*nxt, 2 * i + 1)
                        if i == 1 and not (first and b == 0):
                            output(*prev)

            for m in range(4):
                rotate(0, 0, m)
            group(0, first=True)
            with dve.Fori(1, HP - 1) as hp:
                group(hp)
            group(HP - 1, final=True)
            evacuate(HP - 1, B - 1, QT - 1)
            output(HP - 1, B - 1)

            for b in range(B):
                for hp in range(HP):
                    n = b * HP + hp
                    dve.wait_ge(ot_h, n + 1)
                    v.tensor_tensor(ot_lo[:, hp, :], bank[n % 4][:, :], ot_hi[:, hp, :], ALU.subtract).then_inc(ot_l, 1)
                dve.wait_ge(wo_mm, b + 1)
                mid = o_mid[b % 2][:, :].rearrange("p (i e) -> p i e", i=QT)
                every = [128, QT, E]
                tiles = x_tok[:, b * QT:(b + 1) * QT, :]
                step(v.scalar_tensor_tensor(mid, bank[4 + b % 2][:, :].rearrange("p (i e) -> p i e", i=QT), 1.0 / WS,
                                            bo_b[:, :].unsqueeze(1).broadcast_to(every), ALU.mult, ALU.add))
                step(v.tensor_tensor(mid, mid, gate_a[:, b, :].unsqueeze(1).broadcast_to(every), ALU.mult))
                v.tensor_tensor(tiles, tiles, mid, ALU.add).then_inc(wo_ev, 1)

            dve.wait_ge(wo_ev, B)
            ln_normalise(1)
            dve.wait_ge(ld_k, 80)
            v.scalar_tensor_tensor(k_w[:, :], k_t[:, :], 2.0, rw_sb[:, :], ALU.mult, ALU.add).then_inc(kw_own, 1)
            v.scalar_tensor_tensor(k_neg[:, :], k_t[:, :], -1.0, k_t[:, :], ALU.mult, ALU.mult).then_inc(kw_done, 1)
            ln_modulate(1)

            dve.wait_ge(logit_mm, 1)
            step(v.tensor_copy(logit[:, :, 0:NX], bank[0][:, 0:NT * NX].rearrange("p (t x) -> p t x", t=NT)))
            for t in range(NT):
                v.max(top[:, t, :], logit[:, t, 0:NX]).then_inc(dve_own, 1)
            own[0] += NT
            dve.wait_ge(dve_own, own[0])
            v.tensor_tensor(gates[:, :, :], logit[:, :, 0:NX], top[:, :, 0:1].broadcast_to([128, NT, NX]),
                            ALU.subtract).then_inc(shifted, 1)
            step(v.memset(top[:, :, TOPK:8], -FAR))
            for t in range(NT):
                v.match_replace(taken[:, t, :], top[:, t, :], logit[:, t, :], FAR).then_inc(dve_own, 1)
            own[0] += NT
            dve.wait_ge(dve_own, own[0])
            step(v.tensor_single_scalar(taken[:, :, 0:NX], taken[:, :, 0:NX], FAR, ALU.is_equal))
            dve.wait_ge(gexp, 1)
            step(v.tensor_tensor(gates[:, :, :], gates[:, :, :], taken[:, :, 0:NX], ALU.mult))
            step(v.reduce_sum(gsum[:, :], gates[:, :, :], AX.X))
            step(v.reciprocal(gsum[:, :], gsum[:, :]))
            v.tensor_tensor(gates[:, :, :], gates[:, :, :], gsum[:, :].unsqueeze(2).broadcast_to([128, NT, NX]),
                            ALU.mult).then_inc(gates_done, 1)
            for b in range(B):
                dve.wait_ge(gt_mm, b + 1)
                v.tensor_copy(gates_t[:, b * S:(b + 1) * S], bank[1 + b][0:NX, :]).then_inc(gt_ev, 1)
            for b in range(B):
                dve.wait_ge(b2_mm, b + 1)
                v.tensor_copy(acc[:, b * QT:(b + 1) * QT, :],
                              bank[1 + b][:, :].rearrange("p (i e) -> p i e", i=QT)).then_inc(acc_set, 1)
            dve.wait_ge(gt_mm, B)
            step(v.tensor_scalar(gates[:, :, :], gates[:, :, :], 1.0 / WS, None, ALU.mult))

            def hidden_split(e, tb):
                n = e * B + tb
                w = tb % 2
                if not (isinstance(n, int) and n < 2):
                    dve.wait_ge(down_mm, n - 1)
                for f in (2, 3, 0, 1):
                    if f < 2:
                        dve.wait_ge(g_hi_a, n * 2 + (f + 1))
                    else:
                        dve.wait_ge(gelu_done, n * FT + (f + 1))
                        v.tensor_copy(g_hi[w][f], g_f32[w][f]).then_inc(g_hi_v, 1)
                        dve.wait_ge(g_hi_v, n * 2 + (f - 1))
                    v.tensor_tensor(g_lo[w][f], g_f32[w][f], g_hi[w][f], ALU.subtract).then_inc(g_split, 1)

            def weigh_output(e, tb):
                n = e * B + tb
                dve.wait_ge(down_mm, n + 1)
                if not (isinstance(n, int) and n < 2):
                    dve.wait_ge(acc_add, n - 1)
                v.tensor_tensor(weighted[tb % 2].rearrange("p (i e) -> p i e", i=QT),
                                bank[4 + tb % 2][:, :].rearrange("p (i e) -> p i e", i=QT),
                                gates[:, tb * QT:(tb + 1) * QT, ds(e, 1)].broadcast_to([128, QT, E]),
                                ALU.mult).then_inc(weigh, 1)

            def expert(e, first=False):
                for tb in range(B):
                    hidden_split(e, tb)
                    if tb:
                        weigh_output(e, tb - 1)
                    elif not first:
                        weigh_output(e - 1, B - 1)

            expert(0, first=True)
            with dve.Fori(1, NX) as e:
                expert(e)
            weigh_output(NX - 1, B - 1)

            for b in range(B):
                tiles = acc[:, b * QT:(b + 1) * QT, :]
                dve.wait_ge(acc_add, B * (NX - 1) + b + 1)
                step(v.tensor_tensor(tiles, tiles, gate_b[:, b, :].unsqueeze(1).broadcast_to([128, QT, E]), ALU.mult))
                v.tensor_tensor(tiles, tiles, x_tok[:, b * QT:(b + 1) * QT, :], ALU.add).then_inc(fin, 1)

        @block.gpsimd
        def _(pool):
            g = nc.gpsimd

            def rsqrt(ln):
                pool.wait_ge(consts, 5)
                pool.wait_ge(ln_var, ln + 1)
                g.tensor_tensor(rstd[:, :], var_e[:, :], half[:, :], ALU.pow).then_inc(ln_rstd, 1)

            def rotated(hp, b, m):
                n = (hp * B + b) * 2 + m
                pool.wait_ge(rot_parts, n * 2 + 2)
                if not (isinstance(n, int) and n < 2):
                    pool.wait_ge(qk_lo_done, n - 1)
                g.tensor_tensor(rot[m][:, :], rot_c[m][:, :], rot_s[m][:, :], ALU.add).then_inc(rot_sum, 1)
                pool.wait_ge(qk_hi_done, n + 1)
                g.tensor_tensor(qk_lo[m][b % 2][:, :], rot[m][:, :], qk_hi[m][b % 2][:, :], ALU.subtract).then_inc(qk_lo_done, 1)

            rsqrt(0)
            for b in range(B):
                for m in range(2):
                    rotated(0, b, m)
            with pool.Fori(1, HP) as hp:
                for b in range(B):
                    for m in range(2):
                        rotated(hp, b, m)
            rsqrt(1)

            def split_weights(e, w):
                pool.wait_ge(consts, 5)
                if not (isinstance(e, int) and e == 0):
                    pool.wait_ge(wx_split, e)
                pool.wait_ge(wx_ld[w], (e - w) * 16 + 32)
                g.tensor_tensor(wx_f32, wx_raw[w], ws_col[:, 0:1].broadcast_to([128, 2 * F]), ALU.mult).then_inc(wx_own, 1)
                pool.wait_ge(wx_own, e + 1)
                pool.wait_ge(wx_hi_done, e + 1)
                g.tensor_tensor(wx_lo[w], wx_f32, wx_hi[w], ALU.subtract).then_inc(wx_split, 1)

            def gather(e, tb):
                n = e * B + tb
                pool.wait_ge(weigh, n + 1)
                part = acc[:, tb * QT:(tb + 1) * QT, :]
                g.tensor_tensor(part, part, weighted[tb % 2].rearrange("p (i e) -> p i e", i=QT), ALU.add).then_inc(acc_add, 1)

            split_weights(0, 0)
            split_weights(1, 1)
            pool.wait_ge(acc_set, B)
            for tb in range(B):
                gather(0, tb)
            with pool.Fori(1, NX // 2) as pair:
                for w in range(2):
                    split_weights(pair * 2 + w, w)
                    for tb in range(B):
                        gather(pair * 2 + w - 1, tb)
            for tb in range(B):
                gather(NX - 1, tb)


_OUTS = [((TOK, E), 'float32')]


def kernel(**inputs):
    import numpy as np
    import concourse.bacc as bacc
    from concourse.bass_utils import run_bass_kernel_spmd

    def arr(name):
        return np.asarray(inputs[name])

    swap = np.arange(H * DH).reshape(-1, 2)[:, ::-1].reshape(-1)
    wq, wk, wv = arr("L0_attn_wq"), arr("L0_attn_wk"), arr("L0_attn_wv")
    bq, bk = arr("L0_attn_bq"), arr("L0_attn_bk")
    laid = {
        "x": arr("L0_attn_x").reshape(TOK, E),
        "c_t": arr("L0_c").T,
        "wmod": arr("L0_wmod"),
        "w_qkv": np.concatenate([w.T for w in (wq, wq[swap], wk, wk[swap], wv)], axis=1),
        "b_qk": np.stack([v.reshape(HP, 128).T for v in (bq, bq[swap], bk, bk[swap])], axis=1),
        "bv_rows": np.broadcast_to(arr("L0_attn_bv"), (128, H * DH)),
        "wo_t": arr("L0_attn_wo").T.reshape(HP, 128, E).transpose(1, 0, 2).reshape(128, HP * E),
        "bo_rows": np.broadcast_to(arr("L0_attn_bo"), (128, E)),
        "keys_t": arr("L0_ffn_keys").T,
        "rw_t": arr("L0_ffn_rw").T,
        "rb_row": arr("L0_ffn_rb").reshape(1, NX),
        "w1_t": arr("L0_ffn_w1").transpose(0, 2, 1),
        "b1_t": arr("L0_ffn_b1").reshape(NX, FT, 128).transpose(2, 0, 1),
        "w2_t": arr("L0_ffn_w2").transpose(0, 2, 1).reshape(NX, FT, 128, E).transpose(0, 2, 1, 3).reshape(NX, 128, FT * E),
        "b2": arr("L0_ffn_b2"),
    }
    theta = np.float64(10000.0) ** (np.arange(0, DH, 2) / DH)
    freqs = np.arange(S, dtype=np.float32)[:, None] * (np.float32(1.0) / theta.astype(np.float32))[None, :]
    angle = np.concatenate([freqs, freqs], axis=1).astype(np.float64).T
    sign = np.where(np.arange(DH) % 2 == 0, -1.0, 1.0)[:, None]
    table = np.stack([np.cos(angle), np.sin(angle) * sign], axis=1) / WS
    laid["cos_sin"] = np.concatenate([table, table], axis=0).astype(np.float32)
    query, key = np.arange(128)[:, None], np.arange(128)[None, :]
    laid["causal"] = np.concatenate([np.zeros((128, S - 128)), np.where(key > query, NEG, 0.0)], axis=1).astype(np.float32)
    laid["identity"] = np.eye(128, dtype=np.float32)

    nc = bacc.Bacc("TRN2", target_bir_lowering=False, num_devices=1)
    arrays, aps = {}, {}
    for name, a in laid.items():
        a = np.ascontiguousarray(a)
        arrays[f"in_{name}"] = a
        aps[name] = nc.dram_tensor(f"in_{name}", a.shape, mybir.dt.from_np(a.dtype), kind="ExternalInput").ap()
    out = nc.dram_tensor("out_0", (TOK, E), mybir.dt.float32, kind="ExternalOutput").ap()
    adaln_block(nc, out=out, **aps)
    got = run_bass_kernel_spmd(nc, [arrays], core_ids=[0])
    return got.results[0]["out_0"].reshape(B, S, E)
```

```python
import concourse.bass as bass
from concourse import mybir
from contextlib import ExitStack

B, S, E = 4, 512, 128
H, DH = 16, 64
HP = H * DH // 128
TOK = B * S
NT = TOK // 128
QT = S // 128
NX, F, TOPK = 16, 512, 4
FT = F // 128
UNITS = HP * B
WS = 16.0
SCORE_SCALE = DH ** -0.5
EPS = 1e-5
NEG = -1.0e30
FAR = 3.0e38


def adaln_block(nc, x, c_t, wmod, w_qkv, b_qk, bv_rows, wo_t, bo_rows, keys_t, rw_t, rb_row, w1_t, b1_t, w2_t, b2,
                cos_sin, causal, identity, out):
    f32, f16 = mybir.dt.float32, mybir.dt.float16
    ALU = mybir.AluOpType
    ACT = mybir.ActivationFunctionType
    AX = mybir.AxisListType
    ds = bass.ds

    with ExitStack() as ctx:
        def sb(name, shape, dt=f32):
            return ctx.enter_context(nc.sbuf_tensor(name, shape, dt))

        def sem(name):
            return ctx.enter_context(nc.semaphore(name))

        x_tok = sb("x_tok", [128, NT, E])
        big = sb("big", [128, UNITS * S])
        vo = big[:, :].rearrange("p (g b i d) -> p g b i d", g=HP, b=B, i=QT)
        w_raw = big[:, 0:5 * 1024]
        xn = big[:, UNITS * S - NT * E:UNITS * S].rearrange("p (t e) -> p t e", t=NT)
        h_f32 = sb("h_f32", [128, TOK])
        h_hi = sb("h_hi", [128, TOK], f16)
        h_lo = sb("h_lo", [128, TOK], f16)
        w_hi = sb("w_hi", [128, 5, 1024], f16)
        w_lo = sb("w_lo", [128, 5, 1024], f16)
        wo_sb = sb("wo_sb", [128, HP, E])
        ident = sb("ident", [128, 128])
        mask = sb("mask", [128, S])
        rope = sb("rope", [128, 2, S])
        bqk = sb("bqk", [128, 4, HP])
        bv_b = sb("bv_b", [128, 1024])
        bo_b = sb("bo_b", [128, E])
        c_col = sb("c_col", [128, B])
        c_tmp = sb("c_tmp", [128, B])
        silu_c = sb("silu_c", [128, B])
        silu_b = sb("silu_b", [128, B, 128])
        wm = sb("wm", [128, 6, 128])
        mod_t = sb("mod_t", [128, 4, B])
        gate_a = sb("gate_a", [128, B, E])
        gate_b = sb("gate_b", [128, B, E])
        sign_t = sb("sign_t", [128, B, E])
        stats = sb("stats", [128, NT, 6])
        mv = sb("mv", [128, NT, 2])
        var_e = sb("var_e", [128, NT])
        rstd = sb("rstd", [128, NT])
        half = sb("half", [128, NT])
        rot_c = [sb(f"rot_c{m}", [128, S]) for m in range(2)]
        rot_s = [sb(f"rot_s{m}", [128, S]) for m in range(2)]
        rot = [sb(f"rot{m}", [128, S]) for m in range(2)]
        ot = sb("ot", [128, HP * S])
        qk = ot[:, :].bitcast(f16).rearrange("p (h m b s) -> p h m b s", h=2, m=2, b=B)
        qk_hi = [[qk[:, 0, m, b, :] for b in range(B)] for m in range(2)]
        qk_lo = [[qk[:, 1, m, b, :] for b in range(B)] for m in range(2)]
        p_sb = [[sb(f"p_sb{s}{a}", [128, S]) for a in range(2)] for s in range(QT)]
        pt_sb = [[sb(f"pt_sb{s}{a}", [128, S]) for a in range(2)] for s in range(2)]
        row_max = [sb(f"row_max{v}", [128, 2 * QT]) for v in range(2)]
        row_sum = [sb(f"row_sum{v}", [128, 2 * QT]) for v in range(2)]
        row_inv = sb("row_inv", [128, QT, 2])
        waited = sb("waited", [128, QT])
        ot_t = [pt_sb[n // 2][n % 2] for n in range(4)]
        o_mid = [sb(f"o_mid{v}", [128, S]) for v in range(2)]
        h_sq = rot_c[0]
        k_t = sb("k_t", [128, NX])
        k_w = sb("k_w", [128, NX])
        rw_sb = sb("rw_sb", [128, NX])
        k_neg = sb("k_neg", [128, NX])
        ones = sb("ones", [128, 128])
        minus = sb("minus", [128, NX])
        rb_sb = sb("rb_sb", [1, NX])
        logit = sb("logit", [128, NT, NX + 4])
        taken = sb("taken", [128, NT, NX + 4])
        top = sb("top", [128, NT, 8])
        gates = sb("gates", [128, NT, NX])
        gsum = sb("gsum", [128, NT])
        gates_t = sb("gates_t", [NX, TOK])
        b2_sb = sb("b2_sb", [NX, E])
        b1_sb = sb("b1_sb", [128, NX, FT])
        b1_now = [sb(f"b1_now{w}", [128, FT]) for w in range(2)]
        ws_col = sb("ws_col", [128, 1])
        acc = ot[:, 0:NT * E].rearrange("p (t e) -> p t e", t=NT)

        at = [0]

        def carve(cols, dt=f32):
            words = cols if dt == f32 else cols // 2
            ap = big[:, at[0]:at[0] + words]
            at[0] += words
            return ap if dt == f32 else ap.bitcast(dt)

        g_f32 = [[carve(S) for _ in range(FT)] for _ in range(2)]
        g_hi = [[carve(S, f16) for _ in range(FT)] for _ in range(2)]
        g_lo = [[carve(S, f16) for _ in range(FT)] for _ in range(2)]
        wx_raw = [carve(2 * F) for _ in range(2)]
        wx_f32 = carve(2 * F)
        wx_hi = [carve(2 * F, f16) for _ in range(2)]
        wx_lo = [carve(2 * F, f16) for _ in range(2)]
        weighted = [carve(S) for _ in range(2)]
        assert at[0] <= UNITS * S - NT * E

        bank = [ctx.enter_context(nc.psum_tensor(f"bank{n}", [128, 512], f32)) for n in range(8)]

        ld_x, ld_c, ld_w, ld_k, ld_b = sem("ld_x"), sem("ld_c"), sem("ld_w"), sem("ld_k"), sem("ld_b")
        consts, silu_e, silu_v, mod_mm, mod_ev = sem("consts"), sem("silu_e"), sem("silu_v"), sem("mod_mm"), sem("mod_ev")
        split_hi, split_lo = sem("split_hi"), sem("split_lo")
        dve_own = sem("dve_own")
        ln_var, ln_rstd, ln_xn, ln_tr, ln_f32, ln_hi, ln_lo = (sem(n) for n in (
            "ln_var", "ln_rstd", "ln_xn", "ln_tr", "ln_f32", "ln_hi", "ln_lo"))
        v_mm, v_ev = sem("v_mm"), sem("v_ev")
        proj_mm, rot_parts, rot_sum, qk_hi_done, qk_lo_done = (sem(n) for n in (
            "proj_mm", "rot_parts", "rot_sum", "qk_hi_done", "qk_lo_done"))
        score_mm, masked, exp_done, pt_mm, pt_a, pt_b, pv_mm, o_ev = (sem(n) for n in (
            "score_mm", "masked", "exp_done", "pt_mm", "pt_a", "pt_b", "pv_mm", "o_ev"))
        ot_mm, wo_mm, wo_ev = sem("ot_mm"), sem("wo_mm"), sem("wo_ev")
        ot_ev = [sem("ot_ev0"), sem("ot_ev1")]
        sq_done, kw_done, logit_mm, logit_ev, shifted, gexp, gates_done, gt_mm, gt_ev, b2_mm, acc_set = (
            sem(n) for n in ("sq_done", "kw_done", "logit_mm", "logit_ev", "shifted", "gexp", "gates_done",
                             "gt_mm", "gt_ev", "b2_mm", "acc_set"))
        wx_ld = [sem("wx_ld0"), sem("wx_ld1")]
        wx_split, wx_own = sem("wx_split"), sem("wx_own")
        up_mm, gelu_done, g_hi_a, g_split, down_mm, weigh, acc_add = (sem(n) for n in (
            "up_mm", "gelu_done", "g_hi_a", "g_split", "down_mm", "weigh", "acc_add"))
        wx_hi_done, b1_here = sem("wx_hi_done"), sem("b1_here")
        o_ev_inv, kw_own, g_hi_v = sem("o_ev_inv"), sem("kw_own"), sem("g_hi_v")
        gate_ev = sem("gate_ev")
        fin, stored = sem("fin"), sem("stored")

        def before(hp, b, i, back):
            g = (b * QT + i) - back
            return (hp, g // QT, g % QT) if g >= 0 else (hp - 1, B + g // QT, g % QT)

        def ahead(hp, b):
            return (hp, b + 2) if b + 2 < B else (hp + 1, b + 2 - B)

        block = ctx.enter_context(nc.Block())

        @block.sync
        def _(sp):
            sp.dma_start(x_tok[:, :, :], x.rearrange("(t p) e -> p t e", p=128)).then_inc(ld_x, 16)
            sp.dma_start(ident[:, :], identity).then_inc(ld_c, 16)
            sp.dma_start(c_col[:, :], c_t).then_inc(ld_c, 16)
            sp.dma_start(wm[:, :, :], wmod.rearrange("p (m e) -> p m e", m=6)).then_inc(ld_c, 16)
            sp.dma_start(w_raw, w_qkv).then_inc(ld_w, 16)
            sp.dma_start(wo_sb[:, :, :], wo_t.rearrange("p (g e) -> p g e", g=HP)).then_inc(ld_w, 16)
            sp.dma_start(bv_b[:, :], bv_rows).then_inc(ld_b, 16)
            sp.dma_start(rope[:, :, :], cos_sin).then_inc(ld_b, 16)
            sp.dma_start(bqk[:, :, :], b_qk).then_inc(ld_b, 16)
            sp.dma_start(mask[:, :], causal).then_inc(ld_b, 16)
            sp.dma_start(bo_b[:, :], bo_rows).then_inc(ld_b, 16)
            sp.dma_start(k_t[:, :], keys_t).then_inc(ld_k, 16)
            sp.dma_start(rw_sb[:, :], rw_t).then_inc(ld_k, 16)
            sp.dma_start(rb_sb[:, :], rb_row).then_inc(ld_k, 16)
            sp.dma_start(b2_sb[:, :], b2).then_inc(ld_k, 16)
            sp.dma_start(b1_sb[:, :, :], b1_t).then_inc(ld_k, 16)
            sp.wait_ge(ot_mm, B * HP)
            for e in range(2):
                sp.dma_start(wx_raw[e][:, 0:F], w1_t[e, :, :]).then_inc(wx_ld[e], 16)
                sp.dma_start(wx_raw[e][:, F:2 * F], w2_t[e, :, :]).then_inc(wx_ld[e], 16)
            with sp.Fori(1, NX // 2) as pair:
                for e in range(2):
                    sp.wait_ge(wx_split, pair * 2 + (e - 1))
                    sp.dma_start(wx_raw[e][:, 0:F], w1_t[ds(pair * 2 + e, 1), :, :].squeeze(0)).then_inc(wx_ld[e], 16)
                    sp.dma_start(wx_raw[e][:, F:2 * F], w2_t[ds(pair * 2 + e, 1), :, :].squeeze(0)).then_inc(wx_ld[e], 16)
            for b in range(B):
                sp.wait_ge(fin, b + 1)
                sp.dma_start(out[b * S:(b + 1) * S, :].rearrange("(t p) e -> p t e", p=128),
                             acc[:, b * QT:(b + 1) * QT, :]).then_inc(stored, 16)
            sp.wait_ge(stored, 16 * B)

        @block.tensor
        def _(pe):
            mm = nc.tensor.matmul

            def three(dst, a_hi, a_lo, b_hi, b_lo, first=True, last=True):
                mm(dst, a_hi, b_hi, start=first, stop=False)
                mm(dst, a_hi, b_lo, start=False, stop=False)
                return mm(dst, a_lo, b_hi, start=False, stop=last)

            pe.wait_ge(ld_c, 48)
            pe.wait_ge(silu_v, 1)
            for n, m in enumerate((0, 1, 3, 4)):
                last = mm(bank[0][:, n * B:(n + 1) * B], wm[:, m, :], silu_c[:, :], start=True, stop=True)
            last.then_inc(mod_mm, 1)
            for n, m in enumerate((2, 5)):
                for b in range(B):
                    last = mm(bank[1 + n][:, b * E:(b + 1) * E], silu_b[:, b, :], wm[:, m, :], start=True, stop=True)
                last.then_inc(mod_mm, 1)

            def ln_transposes(ln):
                for b in range(B):
                    pe.wait_ge(ln_xn, ln * B + b + 1)
                    for i in range(QT):
                        last = nc.tensor.transpose(bank[4 + b][:, i * 128:(i + 1) * 128], xn[:, b * QT + i, :], ident[:, :])
                    last.then_inc(ln_tr, 1)

            ln_transposes(0)

            pe.wait_ge(ln_lo, B)
            pe.wait_ge(split_lo, 5)
            def values_in(b, first=False):
                for i in range(QT):
                    for part in range(2):
                        k = 2 * i + part
                        if not first:
                            pe.wait_ge(v_ev, b * 8 + (k - 7))
                        rows = ds(b * S + i * 128, 128)
                        cols = slice(part * 512, part * 512 + 512)
                        three(bank[k][:, :], h_hi[:, rows], h_lo[:, rows], w_hi[:, 4, cols], w_lo[:, 4, cols]).then_inc(v_mm, 1)

            pe.wait_ge(gate_ev, 2)
            values_in(0, first=True)
            with pe.Fori(1, B) as b:
                values_in(b)

            def project(hp, b, m):
                u = hp * B + b
                if m > 0 or not (isinstance(u, int) and u == 0):
                    pe.wait_ge(rot_parts, u * 4 + m)
                toks = slice(b * S, (b + 1) * S)
                cols = ds(hp * 128, 128)
                three(bank[0][:, :], w_hi[:, m, cols], w_lo[:, m, cols], h_hi[:, toks], h_lo[:, toks]).then_inc(proj_mm, 1)

            def scores(hp, b, i):
                u = hp * B + b
                v = b
                if i == 0:
                    pe.wait_ge(qk_lo_done, u * 2 + 2)
                if i >= 2 or not (isinstance(u, int) and u == 0):
                    pe.wait_ge(masked, u * 8 + 2 * i - 2)
                n = (i + 1) * 128
                parts = ((qk_hi, qk_hi), (qk_hi, qk_lo), (qk_lo, qk_hi))
                for k, (q_part, k_part) in enumerate(parts):
                    for a in range(2):
                        rows = slice(a * 64, a * 64 + 64)
                        last = mm(bank[4 + (i % 2) * 2 + a][:, 0:n], q_part[0][v][rows, i * 128:(i + 1) * 128],
                                  k_part[1][v][rows, 0:n], start=k == 0, stop=k == 2)
                        if k == 2:
                            last.then_inc(score_mm, 1)

            def transposes(hp, b, i):
                u = hp * B + b
                g = u * QT + i
                for a in range(2):
                    pe.wait_ge(exp_done, g * 2 + (a + 1))
                    if i > 0 or not (isinstance(u, int) and u == 0):
                        pe.wait_ge((pt_a, pt_b)[a], g)
                    for j in range(i + 1):
                        last = nc.tensor.transpose(bank[2 + a][:, j * 128:(j + 1) * 128],
                                                   p_sb[i][a][:, j * 128:(j + 1) * 128], ident[:, :])
                    last.then_inc(pt_mm, 1)

            def values(hp, b, i):
                u = hp * B + b
                g = u * QT + i
                pe.wait_ge(pt_a, g + 1)
                pe.wait_ge(pt_b, g + 1)
                if i == 0 and not (isinstance(u, int) and u == 0):
                    pe.wait_ge(o_ev, u)
                for a in range(2):
                    for j in range(i + 1):
                        last = mm(bank[1][:, i * 128 + a * 64:i * 128 + a * 64 + 64],
                                  pt_sb[i % 2][a][:, j * 128:(j + 1) * 128],
                                  big[:, ds(hp * (B * S) + b * S + j * 128 + a * 64, 64)],
                                  start=j == 0, stop=j == i)
                last.then_inc(pv_mm, 1)

            def group(hp, first=False, final=False):
                for b in range(B):
                    for i in range(QT):
                        scores(hp, b, i)
                        if not (final and b >= B - 2):
                            project(*ahead(hp, b), i)
                        if not (first and b == 0 and i < 2):
                            transposes(*before(hp, b, i, 2))
                        if not (first and b == 0 and i < 3):
                            values(*before(hp, b, i, 3))

            pe.wait_ge(v_ev, 2 * NT)
            for b in range(2):
                for m in range(4):
                    project(0, b, m)
            group(0, first=True)
            with pe.Fori(1, HP - 1) as hp:
                group(hp)
            group(HP - 1, final=True)
            transposes(HP - 1, B - 1, QT - 2)
            values(HP - 1, B - 1, QT - 3)
            transposes(HP - 1, B - 1, QT - 1)
            values(HP - 1, B - 1, QT - 2)
            values(HP - 1, B - 1, QT - 1)

            pe.wait_ge(o_ev, UNITS)

            def out_transposes(n):
                b, hp = divmod(n, HP)
                if n >= 4:
                    pe.wait_ge(ot_ev[n % 2], (n - 4) // 2 + 1)
                for i in range(QT):
                    last = nc.tensor.transpose(bank[n % 4][:, i * 128:(i + 1) * 128], vo[:, hp, b, i, :], ident[:, :])
                last.then_inc(ot_mm, 1)

            def out_product(n):
                b, hp = divmod(n, HP)
                pe.wait_ge(ot_ev[n % 2], n // 2 + 1)
                if hp == 0 and b >= 2:
                    pe.wait_ge(wo_ev, b - 1)
                for i in range(QT):
                    toks = slice(i * 128, (i + 1) * 128)
                    last = mm(bank[4 + b % 2][:, toks], ot_t[n % 4][:, toks], wo_sb[:, hp, :],
                              start=hp == 0 and i == 0, stop=hp == HP - 1, skip_group_check=True)
                last.then_inc(wo_mm, 1)

            for n in range(B * HP):
                out_transposes(n)
                if n >= 2:
                    out_product(n - 2)
            out_product(B * HP - 2)
            out_product(B * HP - 1)

            pe.wait_ge(wo_ev, B)
            ln_transposes(1)

            pe.wait_ge(kw_done, 1)
            for t in range(NT):
                if t % QT == 0:
                    pe.wait_ge(ln_f32, B + t // QT + 1)
                    pe.wait_ge(sq_done, t // QT + 1)
                dst = bank[0][:, t * NX:(t + 1) * NX]
                mm(dst, h_f32[:, t * 128:(t + 1) * 128], k_w[:, :], start=True, stop=False)
                mm(dst, (rot_c + rot_s)[t // QT][:, (t % QT) * 128:(t % QT + 1) * 128], minus[:, :], start=False, stop=False)
                mm(dst, ones[:, :], k_neg[:, :], start=False, stop=False)
                last = mm(dst, ones[0:1, :], rb_sb[0:1, :], start=False, stop=True)
            last.then_inc(logit_mm, 1)
            pe.wait_ge(gates_done, 1)
            for b in range(B):
                for i in range(QT):
                    last = nc.tensor.transpose(bank[1 + b][0:NX, i * 128:(i + 1) * 128], gates[:, b * QT + i, :], ident[:, :])
                last.then_inc(gt_mm, 1)
            for b in range(B):
                pe.wait_ge(gt_ev, b + 1)
                for i in range(QT):
                    t = b * QT + i
                    last = mm(bank[1 + b][:, i * 128:(i + 1) * 128], gates_t[:, t * 128:(t + 1) * 128], b2_sb[:, :],
                              start=True, stop=True)
                last.then_inc(b2_mm, 1)

            def up(e, w, tb):
                n = e * B + tb
                toks = slice(tb * S, (tb + 1) * S)
                if tb == 0:
                    pe.wait_ge(wx_split, e + 1)
                for f in range(FT):
                    if not (isinstance(n, int) and n == 0):
                        pe.wait_ge(gelu_done, n * FT + (f + 1 - FT))
                    cols = slice(f * 128, (f + 1) * 128)
                    three(bank[f][:, :], wx_hi[w][:, cols], wx_lo[w][:, cols], h_hi[:, toks], h_lo[:, toks]).then_inc(up_mm, 1)

            def down(e, w, tb):
                n = e * B + tb
                v = tb % 2
                pe.wait_ge(g_split, n * FT + FT)
                pe.wait_ge(g_hi_a, n * 2 + 2)
                if not (isinstance(n, int) and n < 2):
                    pe.wait_ge(weigh, n - 1)
                for i in range(QT):
                    toks = slice(i * 128, (i + 1) * 128)
                    for f in range(FT):
                        cols = slice(F + f * 128, F + (f + 1) * 128)
                        last = three(bank[4 + v][:, toks], g_hi[v][f][:, toks], g_lo[v][f][:, toks],
                                     wx_hi[w][:, cols], wx_lo[w][:, cols], first=f == 0, last=f == FT - 1)
                last.then_inc(down_mm, 1)

            def expert_pair(pair, first=False):
                for w in range(2):
                    for tb in range(B):
                        up(pair * 2 + w, w, tb)
                        if not (first and w == 0 and tb == 0):
                            if tb:
                                down(pair * 2 + w, w, tb - 1)
                            else:
                                down(pair * 2 + w - 1, 1 - w, B - 1)

            pe.wait_ge(acc_set, B)
            pe.wait_ge(ln_lo, 2 * B)
            expert_pair(0, first=True)
            with pe.Fori(1, NX // 2) as pair:
                expert_pair(pair)
            down(NX - 1, 1, B - 1)

        @block.scalar
        def _(act):
            act.wait_ge(ld_c, 48)
            nc.scalar.activation(c_tmp[:, :], c_col[:, :], ACT.Exp, scale=-1.0).then_inc(silu_e, 1)
            act.wait_ge(ld_w, 32)
            for m in range(5):
                nc.scalar.activation(w_hi[:, m, :], w_raw[:, m * 1024:(m + 1) * 1024], ACT.Copy, scale=WS).then_inc(split_hi, 1)

            def ln_split(ln):
                for b in range(B):
                    act.wait_ge(ln_f32, ln * B + b + 1)
                    toks = slice(b * S, (b + 1) * S)
                    nc.scalar.activation(h_hi[:, toks], h_f32[:, toks], ACT.Copy).then_inc(ln_hi, 1)

            ln_split(0)

            def qk_round(hp, b, m):
                act.wait_ge(rot_sum, (hp * B + b) * 2 + (m + 1))
                nc.scalar.activation(qk_hi[m][b], rot[m][:, :], ACT.Copy).then_inc(qk_hi_done, 1)

            def exps(hp, b, i):
                n = (i + 1) * 128
                for a in range(2):
                    k = 2 * i + a
                    act.wait_ge(masked, (hp * B + b) * 8 + (k + 1))
                    nc.scalar.activation(p_sb[i][a][:, 0:n], p_sb[i][a][:, 0:n], ACT.Exp,
                                         bias=row_max[b % 2][:, k:k + 1], scale=-1.0,
                                         accum_out=row_sum[b % 2][:, k:k + 1]).then_inc(exp_done, 1)

            def evacuate(hp, b, i):
                act.wait_ge(pt_mm, ((hp * B + b) * QT + i) * 2 + 1)
                n = (i + 1) * 128
                nc.scalar.activation(pt_sb[i % 2][0][:, 0:n], bank[2][:, 0:n], ACT.Copy).then_inc(pt_a, 1)

            def group(hp, first=False, final=False):
                for b in range(B):
                    for i in range(QT):
                        exps(hp, b, i)
                        if not (first and b == 0 and i < 2):
                            evacuate(*before(hp, b, i, 2))
                        if i == 2 and not (final and b >= B - 2):
                            qk_round(*ahead(hp, b), 0)
                        if i == 0 and not (first and b == 0) and not (final and b == B - 1):
                            qk_round(*((hp, b + 1) if b + 1 < B else (hp + 1, 0)), 1)

            for b in range(2):
                for m in range(2):
                    qk_round(0, b, m)
            group(0, first=True)
            with act.Fori(1, HP - 1) as hp:
                group(hp)
            group(HP - 1, final=True)
            evacuate(HP - 1, B - 1, QT - 2)
            evacuate(HP - 1, B - 1, QT - 1)

            for n in range(0, B * HP, 2):
                act.wait_ge(ot_mm, n + 1)
                if n >= 4:
                    act.wait_ge(wo_mm, n - 3)
                nc.scalar.activation(ot_t[n % 4][:, :], bank[n % 4][:, :], ACT.Copy).then_inc(ot_ev[0], 1)

            ln_split(1)
            for b in range(B):
                nc.scalar.activation((rot_c + rot_s)[b][:, :], h_f32[:, b * S:(b + 1) * S], ACT.Square).then_inc(sq_done, 1)
            act.wait_ge(shifted, 1)
            nc.scalar.activation(gates[:, :, :], gates[:, :, :], ACT.Exp).then_inc(gexp, 1)

            def round_weights(e, w):
                act.wait_ge(wx_ld[w], (e - w) * 16 + 32)
                if not (isinstance(e, int) and e < 2):
                    act.wait_ge(down_mm, e * B - B)
                nc.scalar.activation(wx_hi[w], wx_raw[w], ACT.Copy, scale=WS).then_inc(wx_hi_done, 1)

            def hidden(e, w, tb):
                n = e * B + tb
                v = tb % 2
                if tb == 0:
                    act.wait_ge(ld_k, 80)
                    nc.scalar.activation(b1_now[w][:, :], b1_sb[:, ds(e, 1), :].squeeze(1), ACT.Copy).then_inc(b1_here, 1)
                    act.wait_ge(b1_here, e + 1)
                for f in range(FT):
                    act.wait_ge(up_mm, n * FT + (f + 1))
                    if not (isinstance(n, int) and n < 2):
                        act.wait_ge(g_split, n * FT + (f + 1 - 2 * FT))
                    nc.scalar.activation(g_f32[v][f], bank[f][:, :], ACT.Gelu,
                                         bias=b1_now[w][:, f:f + 1], scale=1.0 / WS).then_inc(gelu_done, 1)
                for f in range(2):
                    act.wait_ge(gelu_done, n * FT + (f + 1))
                    if not (isinstance(n, int) and n < 2):
                        act.wait_ge(down_mm, n - 1)
                    nc.scalar.activation(g_hi[v][f], g_f32[v][f], ACT.Copy).then_inc(g_hi_a, 1)

            def expert_pair(pair, last=False):
                for w in range(2):
                    for tb in range(B):
                        hidden(pair * 2 + w, w, tb)
                        if tb == 0 and w == 0 and not (isinstance(pair, int) and pair == 0):
                            round_weights(pair * 2 + 1, 1)
                        if tb == 0 and w == 1 and not last:
                            round_weights(pair * 2 + 2, 0)

            round_weights(0, 0)
            round_weights(1, 1)
            expert_pair(0)
            with act.Fori(1, NX // 2 - 1) as pair:
                expert_pair(pair)
            expert_pair(NX // 2 - 1, last=True)

        @block.vector
        def _(dve):
            own = [0]

            def step(ins):
                own[0] += 1
                ins.then_inc(dve_own, 1)
                dve.wait_ge(dve_own, own[0])

            v = nc.vector
            v.memset(ones[:, :], 1.0).then_inc(consts, 1)
            v.memset(minus[:, :], -1.0).then_inc(consts, 1)
            v.memset(half[:, :], -0.5).then_inc(consts, 1)
            v.memset(ws_col[:, :], WS).then_inc(consts, 1)
            v.memset(logit[:, :, NX:NX + 4], -FAR).then_inc(consts, 1)
            dve.wait_ge(silu_e, 1)
            step(v.tensor_scalar_add(c_tmp[:, :], c_tmp[:, :], 1.0))
            step(v.reciprocal(c_tmp[:, :], c_tmp[:, :]))
            step(v.tensor_tensor(silu_c[:, :], c_col[:, :], c_tmp[:, :], ALU.mult))
            v.tensor_copy(silu_b[:, :, :], silu_c[:, :].unsqueeze(2).broadcast_to([128, B, 128])).then_inc(silu_v, 1)

            def ln_normalise(ln):
                with dve.Fori(0, NT) as t:
                    v.bn_stats(stats[:, ds(t, 1), :].squeeze(1), x_tok[:, ds(t, 1), :].squeeze(1)).then_inc(dve_own, 1)
                own[0] += NT
                dve.wait_ge(dve_own, own[0])
                for t in range(NT):
                    v.bn_aggr(mv[:, t, :], stats[:, t, :]).then_inc(dve_own, 1)
                own[0] += NT
                dve.wait_ge(dve_own, own[0])
                v.tensor_scalar_add(var_e[:, :], mv[:, :, 1], EPS).then_inc(ln_var, 1)
                dve.wait_ge(ln_rstd, ln + 1)
                for b in range(B):
                    for i in range(QT):
                        t = b * QT + i
                        last = v.tensor_scalar(xn[:, t, :], x_tok[:, t, :], mv[:, t, 0:1], rstd[:, t:t + 1],
                                               ALU.subtract, ALU.mult)
                    last.then_inc(ln_xn, 1)

            def ln_modulate(ln):
                for b in range(B):
                    dve.wait_ge(ln_tr, ln * B + b + 1)
                    toks = slice(b * S, (b + 1) * S)
                    v.tensor_scalar(h_f32[:, toks], bank[4 + b][:, :], mod_t[:, 2 * ln + 1, b:b + 1],
                                    mod_t[:, 2 * ln, b:b + 1], ALU.mult, ALU.add).then_inc(ln_f32, 1)
                for b in range(B):
                    dve.wait_ge(ln_hi, ln * B + b + 1)
                    toks = slice(b * S, (b + 1) * S)
                    v.tensor_tensor(h_lo[:, toks], h_f32[:, toks], h_hi[:, toks], ALU.subtract).then_inc(ln_lo, 1)

            dve.wait_ge(ld_x, 16)
            ln_normalise(0)
            dve.wait_ge(mod_mm, 1)
            v.tensor_copy(mod_t[:, :, :], bank[0][:, 0:4 * B].rearrange("p (m b) -> p m b", m=4)).then_inc(mod_ev, 1)
            dve.wait_ge(mod_ev, 1)
            v.tensor_scalar_add(mod_t[:, 1, :], mod_t[:, 1, :], 1.0).then_inc(mod_ev, 1)
            v.tensor_scalar_add(mod_t[:, 3, :], mod_t[:, 3, :], 1.0).then_inc(mod_ev, 1)
            dve.wait_ge(mod_ev, 3)
            ln_modulate(0)
            for n, gate in enumerate((gate_a, gate_b)):
                dve.wait_ge(mod_mm, n + 2)
                src = bank[1 + n][:, :].rearrange("p (b e) -> p b e", b=B)
                step(v.tensor_copy(gate[:, :, :], src))
                step(v.tensor_scalar(sign_t[:, :, :], gate[:, :, :], 0.0, 2.0, ALU.is_ge, ALU.mult))
                step(v.scalar_tensor_tensor(gate[:, :, :], gate[:, :, :], -1.0, gate[:, :, :], ALU.mult, ALU.max))
                step(v.tensor_scalar_max(gate[:, :, :], gate[:, :, :], 0.25))
                v.scalar_tensor_tensor(gate[:, :, :], sign_t[:, :, :], -1.0, gate[:, :, :], ALU.add, ALU.mult).then_inc(gate_ev, 1)
            for m in range(5):
                dve.wait_ge(split_hi, m + 1)
                v.scalar_tensor_tensor(w_lo[:, m, :], w_raw[:, m * 1024:(m + 1) * 1024], WS, w_hi[:, m, :],
                                       ALU.mult, ALU.subtract).then_inc(split_lo, 1)
            dve.wait_ge(ld_b, 80)
            step(v.tensor_scalar(bqk[:, :, :], bqk[:, :, :], WS, None, ALU.mult))
            dve.wait_ge(split_lo, 5)
            dve.wait_ge(ln_xn, B)
            big_v = big[:, :].rearrange("p (g r) -> p g r", g=HP)
            with dve.Fori(0, B) as b:
                for i in range(QT):
                    for part in range(2):
                        dve.wait_ge(v_mm, b * 8 + (2 * i + part + 1))
                        v.scalar_tensor_tensor(
                            big_v[:, part * 4:part * 4 + 4, ds(b * S + i * 128, 128)],
                            bank[2 * i + part][:, :].rearrange("p (g d) -> p g d", g=4), 1.0 / WS,
                            bv_b[:, part * 512:part * 512 + 512].rearrange("p (g d) -> p g d", g=4),
                            ALU.mult, ALU.add).then_inc(v_ev, 1)

            def rotate(hp, b, m):
                u = hp * B + b
                dve.wait_ge(proj_mm, u * 4 + (m + 1))
                if not (isinstance(u, int) and u == 0):
                    dve.wait_ge(rot_sum, u * 2 + (m // 2 - 1))
                dst = (rot_c, rot_s)[m % 2][m // 2]
                v.scalar_tensor_tensor(dst[:, :], bank[0][:, :], bqk[:, m, ds(hp, 1)], rope[:, m % 2, :],
                                       ALU.add, ALU.mult).then_inc(rot_parts, 1)

            def mask_and_max(hp, b, i):
                n = (i + 1) * 128
                dve.wait_ge(score_mm, (hp * B + b) * 8 + (2 * i + 2))
                v.memset(waited[:, i:i + 1], 0.0)
                for a in range(2):
                    k = 2 * i + a
                    v.tensor_tensor_reduce(out=p_sb[i][a][:, 0:n], in0=bank[4 + (i % 2) * 2 + a][:, 0:n],
                                           in1=mask[:, S - n:S], scale=-SCORE_SCALE, scalar=FAR, op0=ALU.add,
                                           op1=ALU.min, accum_out=row_max[b % 2][:, k:k + 1]).then_inc(masked, 1)

            def evacuate(hp, b, i):
                dve.wait_ge(pt_mm, ((hp * B + b) * QT + i) * 2 + 2)
                n = (i + 1) * 128
                v.tensor_copy(pt_sb[i % 2][1][:, 0:n], bank[3][:, 0:n]).then_inc(pt_b, 1)

            def output(hp, b):
                u = hp * B + b
                dve.wait_ge(exp_done, u * 8 + 8)
                v.reciprocal(row_inv[:, :, :], row_sum[b % 2][:, :].rearrange("p (i a) -> p i a", a=2)).then_inc(o_ev_inv, 1)
                dve.wait_ge(o_ev_inv, u + 1)
                dve.wait_ge(pv_mm, u * 4 + 4)
                v.tensor_tensor(big[:, ds(hp * (B * S) + b * S, S)].rearrange("p (i a d) -> p i a d", i=QT, a=2),
                                bank[1][:, :].rearrange("p (i a d) -> p i a d", i=QT, a=2),
                                row_inv[:, :, :].unsqueeze(3).broadcast_to([128, QT, 2, DH]), ALU.mult).then_inc(o_ev, 1)

            def group(hp, first=False, final=False):
                for b in range(B):
                    for i in range(QT):
                        mask_and_max(hp, b, i)
                        if not (final and b >= B - 2):
                            rotate(*ahead(hp, b), i)
                        if not (first and b == 0 and i < 2):
                            evacuate(*before(hp, b, i, 2))
                        if i == 2 and not (first and b == 0):
                            output(*before(hp, b, 0, QT)[:2])

            for b in range(2):
                for m in range(4):
                    rotate(0, b, m)
            group(0, first=True)
            with dve.Fori(1, HP - 1) as hp:
                group(hp)
            group(HP - 1, final=True)
            evacuate(HP - 1, B - 1, QT - 2)
            evacuate(HP - 1, B - 1, QT - 1)
            output(HP - 1, B - 1)

            for b in range(B):
                for n in range(b * HP + 1, (b + 1) * HP, 2):
                    dve.wait_ge(ot_mm, n + 1)
                    if n >= 4:
                        dve.wait_ge(wo_mm, n - 3)
                    v.tensor_copy(ot_t[n % 4][:, :], bank[n % 4][:, :]).then_inc(ot_ev[1], 1)
                dve.wait_ge(wo_mm, (b + 1) * HP)
                mid = o_mid[b % 2][:, :].rearrange("p (i e) -> p i e", i=QT)
                every = [128, QT, E]
                tiles = x_tok[:, b * QT:(b + 1) * QT, :]
                step(v.scalar_tensor_tensor(mid, bank[4 + b % 2][:, :].rearrange("p (i e) -> p i e", i=QT), 0.0,
                                            bo_b[:, :].unsqueeze(1).broadcast_to(every), ALU.add, ALU.add))
                step(v.tensor_tensor(mid, mid, gate_a[:, b, :].unsqueeze(1).broadcast_to(every), ALU.mult))
                v.tensor_tensor(tiles, tiles, mid, ALU.add).then_inc(wo_ev, 1)

            dve.wait_ge(wo_ev, B)
            ln_normalise(1)
            dve.wait_ge(ld_k, 80)
            v.scalar_tensor_tensor(k_w[:, :], k_t[:, :], 2.0, rw_sb[:, :], ALU.mult, ALU.add).then_inc(kw_own, 1)
            v.scalar_tensor_tensor(k_neg[:, :], k_t[:, :], -1.0, k_t[:, :], ALU.mult, ALU.mult).then_inc(kw_done, 1)
            ln_modulate(1)

            dve.wait_ge(logit_mm, 1)
            step(v.tensor_copy(logit[:, :, 0:NX], bank[0][:, 0:NT * NX].rearrange("p (t x) -> p t x", t=NT)))
            for t in range(NT):
                v.max(top[:, t, :], logit[:, t, 0:NX]).then_inc(dve_own, 1)
            own[0] += NT
            dve.wait_ge(dve_own, own[0])
            v.tensor_tensor(gates[:, :, :], logit[:, :, 0:NX], top[:, :, 0:1].broadcast_to([128, NT, NX]),
                            ALU.subtract).then_inc(shifted, 1)
            step(v.memset(top[:, :, TOPK:8], -FAR))
            for t in range(NT):
                v.match_replace(taken[:, t, :], top[:, t, :], logit[:, t, :], FAR).then_inc(dve_own, 1)
            own[0] += NT
            dve.wait_ge(dve_own, own[0])
            step(v.tensor_single_scalar(taken[:, :, 0:NX], taken[:, :, 0:NX], FAR, ALU.is_equal))
            dve.wait_ge(gexp, 1)
            step(v.tensor_tensor(gates[:, :, :], gates[:, :, :], taken[:, :, 0:NX], ALU.mult))
            step(v.reduce_sum(gsum[:, :], gates[:, :, :], AX.X))
            step(v.reciprocal(gsum[:, :], gsum[:, :]))
            v.tensor_tensor(gates[:, :, :], gates[:, :, :], gsum[:, :].unsqueeze(2).broadcast_to([128, NT, NX]),
                            ALU.mult).then_inc(gates_done, 1)
            for b in range(B):
                dve.wait_ge(gt_mm, b + 1)
                v.tensor_copy(gates_t[:, b * S:(b + 1) * S], bank[1 + b][0:NX, :]).then_inc(gt_ev, 1)
            for b in range(B):
                dve.wait_ge(b2_mm, b + 1)
                v.tensor_copy(acc[:, b * QT:(b + 1) * QT, :],
                              bank[1 + b][:, :].rearrange("p (i e) -> p i e", i=QT)).then_inc(acc_set, 1)
            dve.wait_ge(gt_mm, B)
            step(v.tensor_scalar(gates[:, :, :], gates[:, :, :], 1.0 / WS, None, ALU.mult))

            def hidden_split(e, tb):
                n = e * B + tb
                w = tb % 2
                if not (isinstance(n, int) and n < 2):
                    dve.wait_ge(down_mm, n - 1)
                for f in (2, 3, 0, 1):
                    if f < 2:
                        dve.wait_ge(g_hi_a, n * 2 + (f + 1))
                    else:
                        dve.wait_ge(gelu_done, n * FT + (f + 1))
                        v.tensor_copy(g_hi[w][f], g_f32[w][f]).then_inc(g_hi_v, 1)
                        dve.wait_ge(g_hi_v, n * 2 + (f - 1))
                    v.tensor_tensor(g_lo[w][f], g_f32[w][f], g_hi[w][f], ALU.subtract).then_inc(g_split, 1)

            def weigh_output(e, tb):
                n = e * B + tb
                dve.wait_ge(down_mm, n + 1)
                if not (isinstance(n, int) and n < 2):
                    dve.wait_ge(acc_add, n - 1)
                v.tensor_tensor(weighted[tb % 2].rearrange("p (i e) -> p i e", i=QT),
                                bank[4 + tb % 2][:, :].rearrange("p (i e) -> p i e", i=QT),
                                gates[:, tb * QT:(tb + 1) * QT, ds(e, 1)].broadcast_to([128, QT, E]),
                                ALU.mult).then_inc(weigh, 1)

            def expert(e, first=False):
                for tb in range(B):
                    hidden_split(e, tb)
                    if tb:
                        weigh_output(e, tb - 1)
                    elif not first:
                        weigh_output(e - 1, B - 1)

            expert(0, first=True)
            with dve.Fori(1, NX) as e:
                expert(e)
            weigh_output(NX - 1, B - 1)

            for b in range(B):
                tiles = acc[:, b * QT:(b + 1) * QT, :]
                dve.wait_ge(acc_add, B * (NX - 1) + b + 1)
                step(v.tensor_tensor(tiles, tiles, gate_b[:, b, :].unsqueeze(1).broadcast_to([128, QT, E]), ALU.mult))
                v.tensor_tensor(tiles, tiles, x_tok[:, b * QT:(b + 1) * QT, :], ALU.add).then_inc(fin, 1)

        @block.gpsimd
        def _(pool):
            g = nc.gpsimd

            def rsqrt(ln):
                pool.wait_ge(consts, 5)
                pool.wait_ge(ln_var, ln + 1)
                g.tensor_tensor(rstd[:, :], var_e[:, :], half[:, :], ALU.pow).then_inc(ln_rstd, 1)

            def rotated(hp, b, m):
                n = (hp * B + b) * 2 + m
                pool.wait_ge(rot_parts, n * 2 + 2)
                if not (isinstance(n, int) and n < 2):
                    pool.wait_ge(qk_lo_done, n - 1)
                g.tensor_tensor(rot[m][:, :], rot_c[m][:, :], rot_s[m][:, :], ALU.add).then_inc(rot_sum, 1)
                pool.wait_ge(qk_hi_done, n + 1)
                g.tensor_tensor(qk_lo[m][b], rot[m][:, :], qk_hi[m][b], ALU.subtract).then_inc(qk_lo_done, 1)

            rsqrt(0)
            for b in range(B):
                for m in range(2):
                    rotated(0, b, m)
            with pool.Fori(1, HP) as hp:
                for b in range(B):
                    for m in range(2):
                        rotated(hp, b, m)
            rsqrt(1)

            def split_weights(e, w):
                pool.wait_ge(consts, 5)
                if not (isinstance(e, int) and e == 0):
                    pool.wait_ge(wx_split, e)
                pool.wait_ge(wx_ld[w], (e - w) * 16 + 32)
                g.tensor_tensor(wx_f32, wx_raw[w], ws_col[:, 0:1].broadcast_to([128, 2 * F]), ALU.mult).then_inc(wx_own, 1)
                pool.wait_ge(wx_own, e + 1)
                pool.wait_ge(wx_hi_done, e + 1)
                g.tensor_tensor(wx_lo[w], wx_f32, wx_hi[w], ALU.subtract).then_inc(wx_split, 1)

            def gather(e, tb):
                n = e * B + tb
                pool.wait_ge(weigh, n + 1)
                part = acc[:, tb * QT:(tb + 1) * QT, :]
                g.tensor_tensor(part, part, weighted[tb % 2].rearrange("p (i e) -> p i e", i=QT), ALU.add).then_inc(acc_add, 1)

            split_weights(0, 0)
            split_weights(1, 1)
            pool.wait_ge(acc_set, B)
            for tb in range(B):
                gather(0, tb)
            with pool.Fori(1, NX // 2) as pair:
                for w in range(2):
                    split_weights(pair * 2 + w, w)
                    for tb in range(B):
                        gather(pair * 2 + w - 1, tb)
            for tb in range(B):
                gather(NX - 1, tb)


_OUTS = [((TOK, E), 'float32')]


def kernel(**inputs):
    import numpy as np
    import concourse.bacc as bacc
    from concourse.bass_utils import run_bass_kernel_spmd

    def arr(name):
        return np.asarray(inputs[name])

    swap = np.arange(H * DH).reshape(-1, 2)[:, ::-1].reshape(-1)
    wq, wk, wv = arr("L0_attn_wq"), arr("L0_attn_wk"), arr("L0_attn_wv")
    bq, bk = arr("L0_attn_bq"), arr("L0_attn_bk")
    laid = {
        "x": arr("L0_attn_x").reshape(TOK, E),
        "c_t": arr("L0_c").T,
        "wmod": arr("L0_wmod"),
        "w_qkv": np.concatenate([w.T for w in (wq, wq[swap], wk, wk[swap], wv)], axis=1),
        "b_qk": np.stack([v.reshape(HP, 128).T for v in (bq, bq[swap], bk, bk[swap])], axis=1),
        "bv_rows": np.broadcast_to(arr("L0_attn_bv"), (128, H * DH)),
        "wo_t": arr("L0_attn_wo").T.reshape(HP, 128, E).transpose(1, 0, 2).reshape(128, HP * E),
        "bo_rows": np.broadcast_to(arr("L0_attn_bo"), (128, E)),
        "keys_t": arr("L0_ffn_keys").T,
        "rw_t": arr("L0_ffn_rw").T,
        "rb_row": arr("L0_ffn_rb").reshape(1, NX),
        "w1_t": arr("L0_ffn_w1").transpose(0, 2, 1),
        "b1_t": arr("L0_ffn_b1").reshape(NX, FT, 128).transpose(2, 0, 1),
        "w2_t": arr("L0_ffn_w2").transpose(0, 2, 1).reshape(NX, FT, 128, E).transpose(0, 2, 1, 3).reshape(NX, 128, FT * E),
        "b2": arr("L0_ffn_b2"),
    }
    theta = np.float64(10000.0) ** (np.arange(0, DH, 2) / DH)
    freqs = np.arange(S, dtype=np.float32)[:, None] * (np.float32(1.0) / theta.astype(np.float32))[None, :]
    angle = np.concatenate([freqs, freqs], axis=1).astype(np.float64).T
    sign = np.where(np.arange(DH) % 2 == 0, -1.0, 1.0)[:, None]
    table = np.stack([np.cos(angle), np.sin(angle) * sign], axis=1) / WS
    laid["cos_sin"] = np.concatenate([table, table], axis=0).astype(np.float32)
    query, key = np.arange(128)[:, None], np.arange(128)[None, :]
    laid["causal"] = np.concatenate([np.zeros((128, S - 128)), np.where(key > query, NEG, 0.0)], axis=1).astype(np.float32)
    laid["identity"] = np.eye(128, dtype=np.float32)

    nc = bacc.Bacc("TRN2", target_bir_lowering=False, num_devices=1)
    arrays, aps = {}, {}
    for name, a in laid.items():
        a = np.ascontiguousarray(a)
        arrays[f"in_{name}"] = a
        aps[name] = nc.dram_tensor(f"in_{name}", a.shape, mybir.dt.from_np(a.dtype), kind="ExternalInput").ap()
    out = nc.dram_tensor("out_0", (TOK, E), mybir.dt.float32, kind="ExternalOutput").ap()
    adaln_block(nc, out=out, **aps)
    got = run_bass_kernel_spmd(nc, [arrays], core_ids=[0])
    return got.results[0]["out_0"].reshape(B, S, E)
```

```python
import concourse.bass as bass
from concourse import mybir
from contextlib import ExitStack

B, S, E = 4, 512, 128
H, DH = 16, 64
HP = H * DH // 128
TOK = B * S
NT = TOK // 128
QT = S // 128
NX, F, TOPK = 16, 512, 4
FT = F // 128
UNITS = HP * B
WS = 16.0
SCORE_SCALE = DH ** -0.5
EPS = 1e-5
NEG = -1.0e30
FAR = 3.0e38


def adaln_block(nc, x, c_t, wmod, w_qkv, b_qk, bv_t, wo_t, bo_rows, keys_t, rw_t, rb_row, w1_t, b1_t, w2_t, b2,
                cos_sin, causal, identity, out):
    f32, f16 = mybir.dt.float32, mybir.dt.float16
    ALU = mybir.AluOpType
    ACT = mybir.ActivationFunctionType
    AX = mybir.AxisListType
    ds = bass.ds

    with ExitStack() as ctx:
        def sb(name, shape, dt=f32):
            return ctx.enter_context(nc.sbuf_tensor(name, shape, dt))

        def sem(name):
            return ctx.enter_context(nc.semaphore(name))

        x_tok = sb("x_tok", [128, NT, E])
        big = sb("big", [128, UNITS * S])
        vo = big[:, :].rearrange("p (g b i d) -> p g b i d", g=HP, b=B, i=QT)
        w_raw = big[:, 0:3 * 1024]
        xn = big[:, UNITS * S - NT * E:UNITS * S].rearrange("p (t e) -> p t e", t=NT)
        h_f32 = sb("h_f32", [128, TOK])
        h_hi = sb("h_hi", [128, TOK], f16)
        h_lo = sb("h_lo", [128, TOK], f16)
        w_hi = sb("w_hi", [128, 3, 1024], f16)
        w_lo = sb("w_lo", [128, 3, 1024], f16)
        wo_sb = sb("wo_sb", [128, HP, E])
        ident = sb("ident", [128, 128])
        mask = sb("mask", [128, S])
        rope = sb("rope", [128, 2, S])
        bqk = sb("bqk", [128, 2, HP])
        bqk_now = sb("bqk_now", [128, 2])
        bv_col = sb("bv_col", [128, HP])
        bv_wide = sb("bv_wide", [128, HP, 128])
        wo_halves = bv_wide[:, :, :].rearrange("p g e -> p (g e)").bitcast(f16)
        wo_hi, wo_lo = (wo_halves[:, n * HP * E:(n + 1) * HP * E] for n in range(2))
        bo_b = sb("bo_b", [128, E])
        c_col = sb("c_col", [128, B])
        c_tmp = sb("c_tmp", [128, B])
        silu_c = sb("silu_c", [128, B])
        silu_b = sb("silu_b", [128, B, 128])
        wm = sb("wm", [128, 6, 128])
        mod_t = sb("mod_t", [128, 4, B])
        gate_a = sb("gate_a", [128, B, E])
        gate_b = sb("gate_b", [128, B, E])
        sign_t = sb("sign_t", [128, B, E])
        stats = sb("stats", [128, NT, 6])
        mv = sb("mv", [128, NT, 2])
        var_e = sb("var_e", [128, NT])
        rstd = sb("rstd", [128, NT])
        half = sb("half", [128, NT])
        raw = [sb(f"raw{m}", [128, S]) for m in range(2)]
        rot_c = [sb(f"rot_c{m}", [128, S]) for m in range(2)]
        rot_s = [sb(f"rot_s{m}", [128, S]) for m in range(2)]
        rot = [sb(f"rot{m}", [128, S]) for m in range(2)]
        ot = sb("ot", [128, HP * S])
        qk = ot[:, :].bitcast(f16).rearrange("p (h m b s) -> p h m b s", h=2, m=2, b=B)
        qk_hi = [[qk[:, 0, m, b, :] for b in range(B)] for m in range(2)]
        qk_lo = [[qk[:, 1, m, b, :] for b in range(B)] for m in range(2)]
        p_sb = [[sb(f"p_sb{s}{a}", [128, S]) for a in range(2)] for s in range(QT)]
        pt_sb = [[sb(f"pt_sb{s}{a}", [128, S]) for a in range(2)] for s in range(2)]
        row_max = [sb(f"row_max{v}", [128, 2 * QT]) for v in range(2)]
        row_sum = [sb(f"row_sum{v}", [128, 2 * QT]) for v in range(2)]
        row_inv = sb("row_inv", [128, QT, 2])
        waited = sb("waited", [128, QT + 2])
        ot_hi = [pt_sb[n // 2][n % 2][:, :].bitcast(f16)[:, 0:S] for n in range(4)]
        ot_lo = [pt_sb[n // 2][n % 2][:, :].bitcast(f16)[:, S:2 * S] for n in range(4)]
        o_mid = [sb(f"o_mid{v}", [128, S]) for v in range(2)]
        h_sq = rot_c + rot_s
        k_t = sb("k_t", [128, NX])
        k_w = sb("k_w", [128, NX])
        rw_sb = sb("rw_sb", [128, NX])
        k_neg = sb("k_neg", [128, NX])
        ones = sb("ones", [128, 128])
        minus = sb("minus", [128, NX])
        rb_sb = sb("rb_sb", [1, NX])
        logit_c = sb("logit_c", [128, NX])
        logit = sb("logit", [128, NT, NX + 4])
        taken = sb("taken", [128, NT, NX + 4])
        top = sb("top", [128, NT, 8])
        gates = sb("gates", [128, NT, NX])
        gsum = sb("gsum", [128, NT])
        gates_t = sb("gates_t", [NX, TOK])
        b2_sb = sb("b2_sb", [NX, E])
        b1_sb = sb("b1_sb", [128, NX, FT])
        b1_now = [sb(f"b1_now{w}", [128, FT]) for w in range(2)]
        ws_col = sb("ws_col", [128, 1])
        acc = ot[:, 0:NT * E].rearrange("p (t e) -> p t e", t=NT)

        at = [0]

        def carve(cols, dt=f32):
            words = cols if dt == f32 else cols // 2
            ap = big[:, at[0]:at[0] + words]
            at[0] += words
            return ap if dt == f32 else ap.bitcast(dt)

        g_f32 = [[carve(S) for _ in range(FT)] for _ in range(2)]
        g_hi = [[carve(S, f16) for _ in range(FT)] for _ in range(2)]
        g_lo = [[carve(S, f16) for _ in range(FT)] for _ in range(2)]
        wx_raw = [w_hi[:, 0:2, :].rearrange("p m e -> p (m e)").bitcast(f32), carve(2 * F)]
        wx_f32 = w_lo[:, 0:2, :].rearrange("p m e -> p (m e)").bitcast(f32)
        wx_hi = [w_hi[:, 2, :], carve(2 * F, f16)]
        wx_lo = [w_lo[:, 2, :], carve(2 * F, f16)]
        weighted = [carve(S) for _ in range(2)]
        assert at[0] <= UNITS * S - NT * E

        bank = [ctx.enter_context(nc.psum_tensor(f"bank{n}", [128, 512], f32)) for n in range(8)]

        ld_c, ld_wm, ld_k, ld_b = sem("ld_c"), sem("ld_wm"), sem("ld_k"), sem("ld_b")
        consts, silu_e, silu_v, mod_mm, mod_ev = sem("consts"), sem("silu_e"), sem("silu_v"), sem("mod_mm"), sem("mod_ev")
        split_hi, split_lo = sem("split_hi"), sem("split_lo")
        dve_own = sem("dve_own")
        ln_var, ln_rstd, ln_xn, ln_tr, ln_f32, ln_hi, ln_lo = (sem(n) for n in (
            "ln_var", "ln_rstd", "ln_xn", "ln_tr", "ln_f32", "ln_hi", "ln_lo"))
        ld_x = [sem(f"ld_x{b}") for b in range(B)]
        v_mm, v_ev_a, v_ev_v = sem("v_mm"), sem("v_ev_a"), sem("v_ev_v")
        ld_wv, ld_wqk, ld_wo, ld_bv = sem("ld_wv"), sem("ld_wqk"), sem("ld_wo"), sem("ld_bv")
        bv_here, bvwo_mm, bo_done, wo_hi_done, wo_lo_done = (sem(n) for n in (
            "bv_here", "bvwo_mm", "bo_done", "wo_hi_done", "wo_lo_done"))
        gate_here = sem("gate_here")
        proj_mm, raw_done, bias_here, swapped, sin_done, cos_done, rot_sum, qk_hi_done, qk_lo_done = (sem(n) for n in (
            "proj_mm", "raw_done", "bias_here", "swapped", "sin_done", "cos_done", "rot_sum", "qk_hi_done", "qk_lo_done"))
        score_mm, masked, exp_done, pt_mm, pt_a, pt_b, pv_mm, o_ev = (sem(n) for n in (
            "score_mm", "masked", "exp_done", "pt_mm", "pt_a", "pt_b", "pv_mm", "o_ev"))
        ot_mm, wo_mm, wo_ev = sem("ot_mm"), sem("wo_mm"), sem("wo_ev")
        ot_hi_done, ot_lo_done = sem("ot_hi_done"), sem("ot_lo_done")
        sq_done, kw_done, logit_mm, logit_ev, shifted, gexp, gates_done, gt_mm, gt_ev, b2_mm, acc_set = (
            sem(n) for n in ("sq_done", "kw_done", "logit_mm", "logit_ev", "shifted", "gexp", "gates_done",
                             "gt_mm", "gt_ev", "b2_mm", "acc_set"))
        wx_ld = [sem("wx_ld0"), sem("wx_ld1")]
        wx_split, wx_own = sem("wx_split"), sem("wx_own")
        up_mm, gelu_done, g_hi_a, g_split, down_mm, weigh, acc_add = (sem(n) for n in (
            "up_mm", "gelu_done", "g_hi_a", "g_split", "down_mm", "weigh", "acc_add"))
        wx_hi_done, b1_here = sem("wx_hi_done"), sem("b1_here")
        o_ev_inv, kw_own, g_hi_v = sem("o_ev_inv"), sem("kw_own"), sem("g_hi_v")
        o_biased, o_gated = sem("o_biased"), sem("o_gated")
        b2_ws, logit_c_mm, logit_c_done = sem("b2_ws"), sem("logit_c_mm"), sem("logit_c_done")
        fin, stored = sem("fin"), sem("stored")

        def before(hp, b, i, back):
            g = (b * QT + i) - back
            return (hp, g // QT, g % QT) if g >= 0 else (hp - 1, B + g // QT, g % QT)

        LAG = 3

        def ahead(hp, b):
            return (hp, b + 2) if b + 2 < B else (hp + 1, b + 2 - B)

        block = ctx.enter_context(nc.Block())

        @block.sync
        def _(sp):
            sp.dma_start(c_col[:, :], c_t).then_inc(ld_c, 16)
            for b in range(B):
                sp.dma_start(x_tok[:, b * QT:(b + 1) * QT, :],
                             x[b * S:(b + 1) * S, :].rearrange("(t p) e -> p t e", p=128)).then_inc(ld_x[b], 16)
                if b == 0:
                    sp.dma_start(ident[:, :], identity).then_inc(ld_wm, 16)
                    sp.dma_start(wm[:, :, :], wmod.rearrange("p (m e) -> p m e", m=6)).then_inc(ld_wm, 16)
            sp.dma_start(w_raw[:, 2048:3072], w_qkv[:, 2048:3072]).then_inc(ld_wv, 16)
            sp.dma_start(bv_col[:, :], bv_t).then_inc(ld_bv, 16)
            sp.dma_start(bo_b[:, :], bo_rows).then_inc(ld_bv, 16)
            sp.dma_start(wo_sb[:, :, :], wo_t.rearrange("p (g e) -> p g e", g=HP)).then_inc(ld_wo, 16)
            sp.dma_start(w_raw[:, 0:2048], w_qkv[:, 0:2048]).then_inc(ld_wqk, 16)
            sp.dma_start(rope[:, :, :], cos_sin).then_inc(ld_b, 16)
            sp.dma_start(bqk[:, :, :], b_qk).then_inc(ld_b, 16)
            sp.dma_start(mask[:, :], causal).then_inc(ld_b, 16)
            sp.dma_start(k_t[:, :], keys_t).then_inc(ld_k, 16)
            sp.dma_start(rw_sb[:, :], rw_t).then_inc(ld_k, 16)
            sp.dma_start(rb_sb[:, :], rb_row).then_inc(ld_k, 16)
            sp.dma_start(b2_sb[:, :], b2).then_inc(ld_k, 16)
            sp.dma_start(b1_sb[:, :, :], b1_t).then_inc(ld_k, 16)
            for e in range(2):
                if e == 0:
                    sp.wait_ge(proj_mm, 2 * UNITS)
                else:
                    sp.wait_ge(ot_mm, B * HP)
                sp.dma_start(wx_raw[e][:, 0:F], w1_t[e, :, :]).then_inc(wx_ld[e], 16)
                sp.dma_start(wx_raw[e][:, F:2 * F], w2_t[e, :, :]).then_inc(wx_ld[e], 16)
            with sp.Fori(1, NX // 2) as pair:
                for e in range(2):
                    sp.wait_ge(wx_split, pair * 2 + (e - 1))
                    sp.dma_start(wx_raw[e][:, 0:F], w1_t[ds(pair * 2 + e, 1), :, :].squeeze(0)).then_inc(wx_ld[e], 16)
                    sp.dma_start(wx_raw[e][:, F:2 * F], w2_t[ds(pair * 2 + e, 1), :, :].squeeze(0)).then_inc(wx_ld[e], 16)
            for b in range(B):
                sp.wait_ge(fin, b + 1)
                sp.dma_start(out[b * S:(b + 1) * S, :].rearrange("(t p) e -> p t e", p=128),
                             acc[:, b * QT:(b + 1) * QT, :]).then_inc(stored, 16)
            sp.wait_ge(stored, 16 * B)

        @block.tensor
        def _(pe):
            mm = nc.tensor.matmul

            def three(dst, a_hi, a_lo, b_hi, b_lo, first=True, last=True):
                mm(dst, a_hi, b_hi, start=first, stop=False)
                mm(dst, a_hi, b_lo, start=False, stop=False)
                return mm(dst, a_lo, b_hi, start=False, stop=last)

            pe.wait_ge(ld_wm, 32)
            pe.wait_ge(silu_v, 1)
            for n, m in enumerate((0, 1, 3, 4)):
                last = mm(bank[0][:, n * B:(n + 1) * B], wm[:, m, :], silu_c[:, :], start=True, stop=True)
            last.then_inc(mod_mm, 1)
            for n, m in enumerate((2, 5)):
                for b in range(B):
                    last = mm(bank[1 + n][:, b * E:(b + 1) * E], silu_b[:, b, :], wm[:, m, :], start=True, stop=True)
                last.then_inc(mod_mm, 1)

            def ln_transposes(ln, b):
                pe.wait_ge(ln_xn, ln * B + b + 1)
                if ln == 1 and b:
                    pe.wait_ge(ln_f32, B + b)
                for i in range(QT):
                    last = nc.tensor.transpose(bank[6 if ln else 4 + b][:, i * 128:(i + 1) * 128],
                                               xn[:, b * QT + i, :], ident[:, :])
                last.then_inc(ln_tr, 1)

            for b in range(B):
                ln_transposes(0, b)

            pe.wait_ge(bv_here, 1)
            pe.wait_ge(ld_wo, 16)
            for hp in range(HP):
                last = mm(bank[3][:, 0:E], bv_wide[:, hp, :], wo_sb[:, hp, :], start=hp == 0, stop=hp == HP - 1)
            last.then_inc(bvwo_mm, 1)

            def project(hp, b, m):
                u = hp * B + b
                if m > 0 or not (isinstance(u, int) and u == 0):
                    pe.wait_ge(raw_done, u * 2 + m)
                toks = slice(b * S, (b + 1) * S)
                cols = ds(hp * 128, 128)
                three(bank[0][:, :], w_hi[:, m, cols], w_lo[:, m, cols], h_hi[:, toks], h_lo[:, toks]).then_inc(proj_mm, 1)

            pe.wait_ge(split_lo, 1)
            for b in range(B):
                pe.wait_ge(ln_lo, b + 1)
                for k in range(8):
                    i, part = k // 2, k % 2
                    if b:
                        pe.wait_ge((v_ev_a, v_ev_v)[part], (b - 1) * QT + i + 1)
                        if k == 0:
                            pe.wait_ge(raw_done, b)
                    elif k == 0:
                        pe.wait_ge(mod_ev, 1)
                    elif k <= 2:
                        pe.wait_ge(gate_here, k)
                    elif k == 3:
                        pe.wait_ge(bo_done, 1)
                    else:
                        pe.wait_ge(ln_f32, k - 3)
                    rows = slice(b * S + i * 128, b * S + (i + 1) * 128)
                    cols = slice(part * 512, part * 512 + 512)
                    three(bank[k][:, :], h_hi[:, rows], h_lo[:, rows], w_hi[:, 2, cols], w_lo[:, 2, cols]).then_inc(v_mm, 1)
                    if k == 3:
                        pe.wait_ge(split_lo, 3)
                        pe.wait_ge(v_ev_a, b * QT + 1)
                        project(0, b // 2, b % 2)

            def scores(hp, b, i):
                u = hp * B + b
                v = b
                if i == 0:
                    pe.wait_ge(qk_lo_done, u * 2 + 2)
                if i >= 2 or not (isinstance(u, int) and u == 0):
                    pe.wait_ge(masked, u * 8 + 2 * i - 2)
                n = (i + 1) * 128
                parts = ((qk_hi, qk_hi), (qk_hi, qk_lo), (qk_lo, qk_hi))
                for k, (q_part, k_part) in enumerate(parts):
                    for a in range(2):
                        rows = slice(a * 64, a * 64 + 64)
                        last = mm(bank[4 + (i % 2) * 2 + a][:, 0:n], q_part[0][v][rows, i * 128:(i + 1) * 128],
                                  k_part[1][v][rows, 0:n], start=k == 0, stop=k == 2)
                        if k == 2:
                            last.then_inc(score_mm, 1)

            def transposes(hp, b, i):
                u = hp * B + b
                g = u * QT + i
                for a in range(2):
                    pe.wait_ge(exp_done, g * 2 + (a + 1))
                    if i > 0 or not (isinstance(u, int) and u == 0):
                        pe.wait_ge((pt_a, pt_b)[a], g)
                    for j in range(i + 1):
                        last = nc.tensor.transpose(bank[2 + a][:, j * 128:(j + 1) * 128],
                                                   p_sb[i][a][:, j * 128:(j + 1) * 128], ident[:, :])
                    last.then_inc(pt_mm, 1)

            def values(hp, b, i):
                u = hp * B + b
                g = u * QT + i
                pe.wait_ge(pt_a, g + 1)
                pe.wait_ge(pt_b, g + 1)
                if i == 0 and not (isinstance(u, int) and u == 0):
                    pe.wait_ge(o_ev, u)
                for a in range(2):
                    for j in range(i + 1):
                        last = mm(bank[1][:, i * 128 + a * 64:i * 128 + a * 64 + 64],
                                  pt_sb[i % 2][a][:, j * 128:(j + 1) * 128],
                                  big[:, ds(hp * (B * S) + b * S + j * 128 + a * 64, 64)],
                                  start=j == 0, stop=j == i)
                last.then_inc(pv_mm, 1)

            def group(hp, first=False, final=False):
                for b in range(B):
                    for i in range(QT):
                        scores(hp, b, i)
                        if i % 2 == 0 and not (final and b >= B - 2):
                            project(*ahead(hp, b), i // 2)
                        if i == 1 and not (first and b == 0):
                            values(*before(hp, b, i, LAG + 2))
                        if not (first and b == 0 and i < LAG):
                            transposes(*before(hp, b, i, LAG))
                        if i > 0 and not (first and b == 0):
                            values(*before(hp, b, i, LAG + 1))

            pe.wait_ge(v_ev_a, NT)
            pe.wait_ge(v_ev_v, NT)
            group(0, first=True)
            with pe.Fori(1, HP - 1) as hp:
                group(hp)
            group(HP - 1, final=True)
            for i in range(QT - LAG, QT):
                transposes(HP - 1, B - 1, i)
                values(HP - 1, B - 1, i - 1)
            values(HP - 1, B - 1, QT - 1)

            pe.wait_ge(o_ev, UNITS)

            def out_transposes(n):
                b, hp = divmod(n, HP)
                if n >= 4:
                    pe.wait_ge(ot_lo_done, n - 3)
                for i in range(QT):
                    last = nc.tensor.transpose(bank[n % 4][:, i * 128:(i + 1) * 128], vo[:, hp, b, i, :], ident[:, :])
                last.then_inc(ot_mm, 1)

            def out_product(n):
                b, hp = divmod(n, HP)
                pe.wait_ge(wo_lo_done, 1)
                pe.wait_ge(ot_lo_done, n + 1)
                if hp == 0 and b >= 2:
                    pe.wait_ge(o_biased, b - 1)
                for i in range(QT):
                    toks = slice(i * 128, (i + 1) * 128)
                    cols = slice(hp * E, (hp + 1) * E)
                    parts = ((ot_hi, wo_hi), (ot_hi, wo_lo), (ot_lo, wo_hi))
                    for k, (o_part, w_part) in enumerate(parts):
                        last = mm(bank[4 + b % 2][:, toks], o_part[n % 4][:, toks], w_part[:, cols],
                                  start=hp == 0 and i == 0 and k == 0, stop=hp == HP - 1 and k == 2, skip_group_check=True)
                last.then_inc(wo_mm, 1)

            def logits(b):
                pe.wait_ge(logit_c_done, 1)
                pe.wait_ge(ln_f32, B + b + 1)
                pe.wait_ge(sq_done, b + 1)
                for t in range(b * QT, (b + 1) * QT):
                    dst = bank[7][:, t * NX:(t + 1) * NX]
                    own = slice((t % QT) * 128, (t % QT + 1) * 128)
                    mm(dst, h_f32[:, t * 128:(t + 1) * 128], k_w[:, :], start=True, stop=False)
                    last = mm(dst, h_sq[b][:, own], minus[:, :], start=False, stop=True)
                last.then_inc(logit_mm, 1)

            def gate_transposes(b):
                pe.wait_ge(gates_done, b + 1)
                if b:
                    pe.wait_ge(gt_ev, b)
                for i in range(QT):
                    last = nc.tensor.transpose(bank[6][0:NX, i * 128:(i + 1) * 128], gates[:, b * QT + i, :], ident[:, :])
                last.then_inc(gt_mm, 1)

            def output_bias(b):
                pe.wait_ge(gt_ev, b + 1)
                if b:
                    pe.wait_ge(acc_set, b)
                else:
                    pe.wait_ge(b2_ws, 1)
                    pe.wait_ge(shifted, B)
                for i in range(QT):
                    t = b * QT + i
                    last = mm(bank[7][:, i * 128:(i + 1) * 128], gates_t[:, t * 128:(t + 1) * 128], b2_sb[:, :],
                              start=True, stop=True)
                last.then_inc(b2_mm, 1)

            for k in range(B):
                for j in range(HP):
                    if k == 0 and j == 3:
                        pe.wait_ge(kw_done, 1)
                        mm(bank[7][:, 0:NX], ones[:, :], k_neg[:, :], start=True, stop=False)
                        mm(bank[7][:, 0:NX], ones[0:1, :], rb_sb[0:1, :], start=False, stop=True).then_inc(logit_c_mm, 1)
                    out_transposes(k * HP + j)
                    if k or j >= 3:
                        out_product(k * HP + j - 3)
                    if j == 1 and k >= 2:
                        ln_transposes(1, k - 2)
                    if j == 3 and k >= 2:
                        logits(k - 2)
            for n in range(B * HP - 3, B * HP):
                out_product(n)
            ln_transposes(1, B - 2)

            def up(e, w, tb):
                n = e * B + tb
                toks = slice(tb * S, (tb + 1) * S)
                if tb == 0:
                    pe.wait_ge(wx_split, e + 1)
                for f in range(FT):
                    if not (isinstance(n, int) and n == 0):
                        pe.wait_ge(gelu_done, n * FT + (f + 1 - FT))
                    cols = slice(f * 128, (f + 1) * 128)
                    three(bank[f][:, :], wx_hi[w][:, cols], wx_lo[w][:, cols], h_hi[:, toks], h_lo[:, toks]).then_inc(up_mm, 1)

            def down(e, w, tb):
                n = e * B + tb
                v = tb % 2
                pe.wait_ge(g_split, n * FT + FT)
                pe.wait_ge(g_hi_a, n * 2 + 2)
                if not (isinstance(n, int) and n < 2):
                    pe.wait_ge(weigh, n - 1)
                for i in range(QT):
                    toks = slice(i * 128, (i + 1) * 128)
                    for f in range(FT):
                        cols = slice(F + f * 128, F + (f + 1) * 128)
                        last = three(bank[4 + v][:, toks], g_hi[v][f][:, toks], g_lo[v][f][:, toks],
                                     wx_hi[w][:, cols], wx_lo[w][:, cols], first=f == 0, last=f == FT - 1)
                last.then_inc(down_mm, 1)

            def expert_pair(pair, first=False):
                for w in range(2):
                    for tb in range(B):
                        n = w * B + tb
                        if first and 2 <= n < 2 + B:
                            gate_transposes(n - 2)
                        if first and w == 0:
                            pe.wait_ge(ln_lo, B + tb + 1)
                        up(pair * 2 + w, w, tb)
                        if first and n == 0:
                            logits(B - 2)
                            ln_transposes(1, B - 1)
                            continue
                        if first and n == 1:
                            logits(B - 1)
                        if tb:
                            down(pair * 2 + w, w, tb - 1)
                        else:
                            down(pair * 2 + w - 1, 1 - w, B - 1)
                        if first and 2 <= n < 2 + B:
                            output_bias(n - 2)

            expert_pair(0, first=True)
            with pe.Fori(1, NX // 2) as pair:
                expert_pair(pair)
            down(NX - 1, 1, B - 1)

        @block.scalar
        def _(act):
            act.wait_ge(ld_c, 16)
            nc.scalar.activation(c_tmp[:, :], c_col[:, :], ACT.Exp, scale=-1.0).then_inc(silu_e, 1)
            act.wait_ge(ld_wv, 16)
            nc.scalar.activation(w_hi[:, 2, :], w_raw[:, 2048:3072], ACT.Copy, scale=WS).then_inc(split_hi, 1)
            for n, gate in enumerate((gate_a, gate_b)):
                act.wait_ge(mod_mm, n + 2)
                nc.scalar.activation(gate[:, :, :], bank[1 + n][:, :].rearrange("p (b e) -> p b e", b=B),
                                     ACT.Copy).then_inc(gate_here, 1)

            def ln_round(ln, b):
                act.wait_ge(ln_f32, ln * B + b + 1)
                toks = slice(b * S, (b + 1) * S)
                nc.scalar.activation(h_hi[:, toks], h_f32[:, toks], ACT.Copy).then_inc(ln_hi, 1)

            ln_round(0, 0)
            act.wait_ge(ld_wqk, 16)
            for m in range(2):
                nc.scalar.activation(w_hi[:, m, :], w_raw[:, m * 1024:(m + 1) * 1024], ACT.Copy, scale=WS).then_inc(split_hi, 1)
            for b in range(1, B):
                ln_round(0, b)

            def qk_round(hp, b, m):
                act.wait_ge(rot_sum, (hp * B + b) * 2 + (m + 1))
                nc.scalar.activation(qk_hi[m][b], rot[m][:, :], ACT.Copy).then_inc(qk_hi_done, 1)

            def fetch_bias(hp):
                nc.scalar.activation(bqk_now[:, :], bqk[:, :, ds(hp, 1)].squeeze(2), ACT.Copy).then_inc(bias_here, 1)

            def unscale(hp, b, m):
                u = hp * B + b
                act.wait_ge(bias_here, hp + 1)
                if not (isinstance(u, int) and u == 0):
                    act.wait_ge(rot_sum, u * 2 + (m - 1))
                act.wait_ge(proj_mm, u * 2 + (m + 1))
                nc.scalar.activation(raw[m][:, :], bank[0][:, :], ACT.Identity, bias=bqk_now[:, m:m + 1],
                                     scale=1.0 / WS).then_inc(raw_done, 1)

            def exps(hp, b, i):
                n = (i + 1) * 128
                for a in range(2):
                    k = 2 * i + a
                    act.wait_ge(masked, (hp * B + b) * 8 + (k + 1))
                    nc.scalar.activation(p_sb[i][a][:, 0:n], p_sb[i][a][:, 0:n], ACT.Exp,
                                         bias=row_max[b % 2][:, k:k + 1], scale=-1.0,
                                         accum_out=row_sum[b % 2][:, k:k + 1]).then_inc(exp_done, 1)

            def evacuate(hp, b, i):
                act.wait_ge(pt_mm, ((hp * B + b) * QT + i) * 2 + 1)
                n = (i + 1) * 128
                nc.scalar.activation(pt_sb[i % 2][0][:, 0:n], bank[2][:, 0:n], ACT.Copy).then_inc(pt_a, 1)

            def group(hp, first=False, final=False):
                for b in range(B):
                    for i in range(QT):
                        if i:
                            exps(hp, b, i)
                        if not (first and b == 0 and i < LAG):
                            evacuate(*before(hp, b, i, LAG))
                        if i == 0:
                            exps(hp, b, i)
                        if i == 0 and b == 2 and not final:
                            fetch_bias(hp + 1)
                        if i % 2 == 0 and not (final and b >= B - 2):
                            unscale(*ahead(hp, b), i // 2)
                        if i == 3 and not (final and b >= B - 2):
                            qk_round(*ahead(hp, b), 0)
                        if i == 1 and not (final and b == B - 1):
                            qk_round(*((hp, b + 1) if b + 1 < B else (hp + 1, 0)), 1)

            act.wait_ge(ld_b, 48)
            fetch_bias(0)
            act.wait_ge(bvwo_mm, 1)
            nc.scalar.activation(wo_hi, wo_sb[:, :, :].rearrange("p g e -> p (g e)"), ACT.Copy, scale=WS).then_inc(wo_hi_done, 1)
            big_v = big[:, :].rearrange("p (g r) -> p g r", g=HP)
            for b in range(B):
                for i in range(QT):
                    act.wait_ge(split_lo, 3)
                    act.wait_ge(v_mm, b * 8 + 2 * i + 1)
                    nc.scalar.activation(big_v[:, 0:4, b * S + i * 128:b * S + (i + 1) * 128],
                                         bank[2 * i][:, :].rearrange("p (g d) -> p g d", g=4), ACT.Copy,
                                         scale=1.0 / WS).then_inc(v_ev_a, 1)
                    if i == 1:
                        unscale(0, b // 2, b % 2)
                        if b:
                            qk_round(0, (b - 1) // 2, (b - 1) % 2)
            group(0, first=True)
            with act.Fori(1, HP - 1) as hp:
                group(hp)
            group(HP - 1, final=True)
            for i in range(QT - LAG, QT):
                evacuate(HP - 1, B - 1, i)

            def round_weights(e, w):
                act.wait_ge(wx_ld[w], (e - w) * 16 + 32)
                if not (isinstance(e, int) and e < 2):
                    act.wait_ge(down_mm, e * B - B)
                nc.scalar.activation(wx_hi[w], wx_raw[w], ACT.Copy, scale=WS).then_inc(wx_hi_done, 1)

            def square(b):
                act.wait_ge(ln_f32, B + b + 1)
                nc.scalar.activation(h_sq[b][:, :], h_f32[:, b * S:(b + 1) * S], ACT.Square).then_inc(sq_done, 1)

            def gate_exp(b):
                act.wait_ge(shifted, b + 1)
                tiles = gates[:, b * QT:(b + 1) * QT, :]
                nc.scalar.activation(tiles, tiles, ACT.Exp).then_inc(gexp, 1)

            round_weights(0, 0)
            for k in range(B):
                for j in range(HP):
                    n = k * HP + j
                    act.wait_ge(ot_mm, n + 1)
                    if n >= 4:
                        act.wait_ge(wo_mm, n - 3)
                    nc.scalar.activation(ot_hi[n % 4], bank[n % 4][:, :], ACT.Copy).then_inc(ot_hi_done, 1)
                    if j == 2 and k >= 2:
                        square(k - 2)
                        ln_round(1, k - 2)
                    if j == 6 and k >= 2:
                        gate_exp(k - 2)
                        if k == B - 1:
                            nc.scalar.activation(c_tmp[:, :], c_col[:, :], ACT.Gelu)
            square(B - 2)
            ln_round(1, B - 2)

            def hidden(e, w, tb):
                n = e * B + tb
                v = tb % 2
                if tb == 0:
                    act.wait_ge(ld_k, 80)
                    nc.scalar.activation(b1_now[w][:, :], b1_sb[:, ds(e, 1), :].squeeze(1), ACT.Copy).then_inc(b1_here, 1)
                    act.wait_ge(b1_here, e + 1)
                for f in range(FT):
                    act.wait_ge(up_mm, n * FT + (f + 1))
                    if not (isinstance(n, int) and n < 2):
                        act.wait_ge(g_split, n * FT + (f + 1 - 2 * FT))
                    nc.scalar.activation(g_f32[v][f], bank[f][:, :], ACT.Gelu,
                                         bias=b1_now[w][:, f:f + 1], scale=1.0 / WS).then_inc(gelu_done, 1)
                for f in range(2):
                    act.wait_ge(gelu_done, n * FT + (f + 1))
                    if not (isinstance(n, int) and n < 2):
                        act.wait_ge(down_mm, n - 1)
                    nc.scalar.activation(g_hi[v][f], g_f32[v][f], ACT.Copy).then_inc(g_hi_a, 1)

            def expert_pair(pair, first=False, last=False):
                for w in range(2):
                    for tb in range(B):
                        hidden(pair * 2 + w, w, tb)
                        if first and w == 0 and tb == 0:
                            square(B - 1)
                            ln_round(1, B - 1)
                        if first and w == 0 and tb == 1:
                            gate_exp(B - 2)
                            gate_exp(B - 1)
                            round_weights(1, 1)
                        if tb == 0 and w == 0 and not (isinstance(pair, int) and pair == 0):
                            round_weights(pair * 2 + 1, 1)
                        if tb == 0 and w == 1 and not last:
                            round_weights(pair * 2 + 2, 0)

            expert_pair(0, first=True)
            with act.Fori(1, NX // 2 - 1) as pair:
                expert_pair(pair)
            expert_pair(NX // 2 - 1, last=True)

        @block.vector
        def _(dve):
            own = [0]

            def step(ins):
                own[0] += 1
                ins.then_inc(dve_own, 1)
                dve.wait_ge(dve_own, own[0])

            v = nc.vector
            v.memset(ones[:, :], 1.0).then_inc(consts, 1)
            v.memset(minus[:, :], -1.0).then_inc(consts, 1)
            v.memset(half[:, :], -0.5).then_inc(consts, 1)
            v.memset(ws_col[:, :], WS).then_inc(consts, 1)
            v.memset(logit[:, :, NX:NX + 4], -FAR).then_inc(consts, 1)
            dve.wait_ge(ld_c, 16)
            dve.wait_ge(silu_e, 1)
            step(v.tensor_scalar_add(c_tmp[:, :], c_tmp[:, :], 1.0))
            step(v.reciprocal(c_tmp[:, :], c_tmp[:, :]))
            step(v.tensor_tensor(silu_c[:, :], c_col[:, :], c_tmp[:, :], ALU.mult))
            v.tensor_copy(silu_b[:, :, :], silu_c[:, :].unsqueeze(2).broadcast_to([128, B, 128])).then_inc(silu_v, 1)

            def ln_statistics(ln, b):
                tiles = range(b * QT, (b + 1) * QT)
                for t in tiles:
                    v.bn_stats(stats[:, t, :], x_tok[:, t, :]).then_inc(dve_own, 1)
                own[0] += QT
                dve.wait_ge(dve_own, own[0])
                for t in tiles:
                    v.bn_aggr(mv[:, t, :], stats[:, t, :]).then_inc(dve_own, 1)
                own[0] += QT
                dve.wait_ge(dve_own, own[0])
                v.tensor_scalar_add(var_e[:, b * QT:(b + 1) * QT], mv[:, b * QT:(b + 1) * QT, 1], EPS).then_inc(ln_var, 1)

            def ln_normalise(ln, b):
                dve.wait_ge(ln_rstd, ln * B + b + 1)
                for t in range(b * QT, (b + 1) * QT):
                    last = v.tensor_scalar(xn[:, t, :], x_tok[:, t, :], mv[:, t, 0:1], rstd[:, t:t + 1],
                                           ALU.subtract, ALU.mult)
                last.then_inc(ln_xn, 1)

            def ln_modulate(ln, b):
                dve.wait_ge(ln_tr, ln * B + b + 1)
                v.tensor_scalar(h_f32[:, b * S:(b + 1) * S], bank[6 if ln else 4 + b][:, :], mod_t[:, 2 * ln + 1, b:b + 1],
                                mod_t[:, 2 * ln, b:b + 1], ALU.mult, ALU.add).then_inc(ln_f32, 1)

            def ln_low(ln, b):
                dve.wait_ge(ln_hi, ln * B + b + 1)
                toks = slice(b * S, (b + 1) * S)
                v.tensor_tensor(h_lo[:, toks], h_f32[:, toks], h_hi[:, toks], ALU.subtract).then_inc(ln_lo, 1)

            def weights_low(m):
                n = (m + 1) % 3
                dve.wait_ge(split_hi, n + 1)
                v.scalar_tensor_tensor(w_lo[:, m, :], w_raw[:, m * 1024:(m + 1) * 1024], WS, w_hi[:, m, :],
                                       ALU.mult, ALU.subtract).then_inc(split_lo, 1)

            for b in range(B):
                dve.wait_ge(ld_x[b], 16)
                ln_statistics(0, b)
                if b:
                    ln_normalise(0, b - 1)
            ln_normalise(0, B - 1)
            dve.wait_ge(ld_bv, 32)
            v.tensor_copy(bv_wide[:, :, :], bv_col[:, :].unsqueeze(2).broadcast_to([128, HP, 128])).then_inc(bv_here, 1)
            dve.wait_ge(mod_mm, 1)
            v.tensor_copy(mod_t[:, :, :], bank[0][:, 0:4 * B].rearrange("p (m b) -> p m b", m=4)).then_inc(mod_ev, 1)
            dve.wait_ge(mod_ev, 1)
            v.tensor_scalar_add(mod_t[:, 1, :], mod_t[:, 1, :], 1.0).then_inc(mod_ev, 1)
            v.tensor_scalar_add(mod_t[:, 3, :], mod_t[:, 3, :], 1.0).then_inc(mod_ev, 1)
            dve.wait_ge(mod_ev, 3)
            ln_modulate(0, 0)
            weights_low(2)
            ln_low(0, 0)
            dve.wait_ge(bvwo_mm, 1)
            v.tensor_tensor(bo_b[:, :], bank[3][:, 0:E], bo_b[:, :], ALU.add).then_inc(bo_done, 1)
            for b in range(1, B):
                ln_modulate(0, b)
            weights_low(0)
            weights_low(1)
            for b in range(1, B):
                ln_low(0, b)
            dve.wait_ge(split_lo, 3)
            dve.wait_ge(ln_tr, B)

            neighbours = [p ^ 1 for p in range(32)]

            def rotate(hp, b, m):
                n = (hp * B + b) * 2 + m
                if not (isinstance(n, int) and n < 2):
                    dve.wait_ge(rot_sum, n - 1)
                dve.wait_ge(raw_done, n + 1)
                v.memset(waited[:, QT + m:QT + m + 1], 0.0)
                v.stream_shuffle(rot_s[m][:, :], raw[m][:, :], neighbours).then_inc(swapped, 1)
                dve.wait_ge(swapped, n + 1)
                v.tensor_tensor(rot_s[m][:, :], rot_s[m][:, :], rope[:, 1, :], ALU.mult).then_inc(sin_done, 1)

            def mask_and_max(hp, b, i):
                n = (i + 1) * 128
                dve.wait_ge(score_mm, (hp * B + b) * 8 + (2 * i + 2))
                v.memset(waited[:, i:i + 1], 0.0)
                for a in range(2):
                    k = 2 * i + a
                    v.tensor_tensor_reduce(out=p_sb[i][a][:, 0:n], in0=bank[4 + (i % 2) * 2 + a][:, 0:n],
                                           in1=mask[:, S - n:S], scale=-SCORE_SCALE, scalar=FAR, op0=ALU.add,
                                           op1=ALU.min, accum_out=row_max[b % 2][:, k:k + 1]).then_inc(masked, 1)

            def evacuate(hp, b, i):
                dve.wait_ge(pt_mm, ((hp * B + b) * QT + i) * 2 + 2)
                n = (i + 1) * 128
                v.tensor_copy(pt_sb[i % 2][1][:, 0:n], bank[3][:, 0:n]).then_inc(pt_b, 1)

            def invert(hp, b):
                u = hp * B + b
                dve.wait_ge(exp_done, u * 8 + 8)
                v.reciprocal(row_inv[:, :, :], row_sum[b % 2][:, :].rearrange("p (i a) -> p i a", a=2)).then_inc(o_ev_inv, 1)

            def output(hp, b):
                u = hp * B + b
                dve.wait_ge(o_ev_inv, u + 1)
                dve.wait_ge(pv_mm, u * 4 + 4)
                v.tensor_tensor(big[:, ds(hp * (B * S) + b * S, S)].rearrange("p (i a d) -> p i a d", i=QT, a=2),
                                bank[1][:, :].rearrange("p (i a d) -> p i a d", i=QT, a=2),
                                row_inv[:, :, :].unsqueeze(3).broadcast_to([128, QT, 2, DH]), ALU.mult).then_inc(o_ev, 1)

            def keep_size(gate):
                step(v.tensor_scalar(sign_t[:, :, :], gate[:, :, :], 0.0, 2.0, ALU.is_ge, ALU.mult))
                step(v.scalar_tensor_tensor(gate[:, :, :], gate[:, :, :], -1.0, gate[:, :, :], ALU.mult, ALU.max))
                step(v.tensor_scalar_max(gate[:, :, :], gate[:, :, :], 0.25))
                step(v.scalar_tensor_tensor(gate[:, :, :], sign_t[:, :, :], -1.0, gate[:, :, :], ALU.add, ALU.mult))

            def prepare(part):
                if part == 0:
                    dve.wait_ge(wo_hi_done, 1)
                    v.scalar_tensor_tensor(wo_lo, wo_sb[:, :, :].rearrange("p g e -> p (g e)"), WS, wo_hi,
                                           ALU.mult, ALU.subtract).then_inc(wo_lo_done, 1)
                elif part == 1:
                    dve.wait_ge(ld_k, 80)
                    v.scalar_tensor_tensor(k_w[:, :], k_t[:, :], 2.0, rw_sb[:, :], ALU.mult, ALU.add).then_inc(kw_own, 1)
                    v.scalar_tensor_tensor(k_neg[:, :], k_t[:, :], -1.0, k_t[:, :], ALU.mult, ALU.mult).then_inc(kw_done, 1)
                    v.tensor_scalar(b2_sb[:, :], b2_sb[:, :], WS, None, ALU.mult).then_inc(b2_ws, 1)
                else:
                    keep_size((gate_a, gate_b)[part - 2])

            def group(hp, first=False, final=False):
                for b in range(B):
                    for i in range(QT):
                        if i == 0 and not (first and b < 2):
                            output(*before(hp, b, 0, 2 * QT)[:2])
                        mask_and_max(hp, b, i)
                        if i == 2 and not (first and b == 0):
                            invert(*before(hp, b, 0, QT)[:2])
                        if not (first and b == 0 and i < LAG):
                            evacuate(*before(hp, b, i, LAG))
                        if i % 2 == 1 and not (final and b >= B - 2):
                            rotate(*ahead(hp, b), i // 2)
                        if i % 2 == 1 and final and b >= B - 2:
                            prepare((b - (B - 2)) * 2 + i // 2)


            big_v = big[:, :].rearrange("p (g r) -> p g r", g=HP)
            for b in range(B):
                for i in range(QT):
                    dve.wait_ge(v_mm, b * 8 + 2 * i + 2)
                    v.tensor_scalar(big_v[:, 4:8, b * S + i * 128:b * S + (i + 1) * 128],
                                    bank[2 * i + 1][:, :].rearrange("p (g d) -> p g d", g=4), 1.0 / WS, None,
                                    ALU.mult).then_inc(v_ev_v, 1)
                    if i == 2:
                        rotate(0, b // 2, b % 2)
            group(0, first=True)
            with dve.Fori(1, HP - 1) as hp:
                group(hp)
            group(HP - 1, final=True)
            output(HP - 1, B - 2)
            for i in range(QT - LAG, QT):
                evacuate(HP - 1, B - 1, i)
            invert(HP - 1, B - 1)
            output(HP - 1, B - 1)

            def add_attention(b):
                dve.wait_ge(wo_mm, (b + 1) * HP)
                if b >= 2:
                    dve.wait_ge(wo_ev, b - 1)
                mid = o_mid[b % 2][:, :].rearrange("p (i e) -> p i e", i=QT)
                every = [128, QT, E]
                tiles = x_tok[:, b * QT:(b + 1) * QT, :]
                v.scalar_tensor_tensor(mid, bank[4 + b % 2][:, :].rearrange("p (i e) -> p i e", i=QT), 1.0 / WS,
                                       bo_b[:, :].unsqueeze(1).broadcast_to(every), ALU.mult, ALU.add).then_inc(o_biased, 1)
                if b == B - 1:
                    dve.wait_ge(o_biased, B)
                    step(v.tensor_tensor(mid, mid, gate_a[:, b, :].unsqueeze(1).broadcast_to(every), ALU.mult))
                    v.tensor_tensor(tiles, tiles, mid, ALU.add).then_inc(wo_ev, 1)

            def choose(b):
                tiles = slice(b * QT, (b + 1) * QT)
                each = range(b * QT, (b + 1) * QT)
                dve.wait_ge(logit_mm, b + 1)
                step(v.tensor_tensor(logit[:, tiles, 0:NX],
                                     bank[7][:, b * QT * NX:(b + 1) * QT * NX].rearrange("p (t x) -> p t x", t=QT),
                                     logit_c[:, :].unsqueeze(1).broadcast_to([128, QT, NX]), ALU.add))
                for t in each:
                    v.max(top[:, t, :], logit[:, t, 0:NX]).then_inc(dve_own, 1)
                own[0] += QT
                dve.wait_ge(dve_own, own[0])
                v.tensor_tensor(gates[:, tiles, :], logit[:, tiles, 0:NX], top[:, tiles, 0:1].broadcast_to([128, QT, NX]),
                                ALU.subtract).then_inc(shifted, 1)
                dve.wait_ge(shifted, b + 1)
                step(v.memset(top[:, tiles, TOPK:8], -FAR))
                for t in each:
                    v.match_replace(taken[:, t, :], top[:, t, :], logit[:, t, :], FAR).then_inc(dve_own, 1)
                own[0] += QT
                dve.wait_ge(dve_own, own[0])
                step(v.tensor_single_scalar(taken[:, tiles, 0:NX], taken[:, tiles, 0:NX], FAR, ALU.is_equal))

            def weights_of(b):
                tiles = slice(b * QT, (b + 1) * QT)
                part, total = gates[:, tiles, :], gsum[:, tiles]
                dve.wait_ge(gexp, b + 1)
                step(v.tensor_tensor(part, part, taken[:, tiles, 0:NX], ALU.mult))
                step(v.reduce_sum(total, part, AX.X))
                step(v.reciprocal(total, total))
                v.scalar_tensor_tensor(part, part, 1.0 / WS, total.unsqueeze(2).broadcast_to([128, QT, NX]),
                                       ALU.mult, ALU.mult).then_inc(gates_done, 1)

            for k in range(B + 1):
                for j in range(HP):
                    n = k * HP + j
                    if k < B:
                        dve.wait_ge(ot_mm, n + 1)
                        if n >= 4:
                            dve.wait_ge(wo_mm, n - 3)
                        dve.wait_ge(ot_hi_done, n + 1)
                        v.tensor_tensor(ot_lo[n % 4], bank[n % 4][:, :], ot_hi[n % 4], ALU.subtract).then_inc(ot_lo_done, 1)
                    if j == 5 and not k:
                        dve.wait_ge(logit_c_mm, 1)
                        v.tensor_copy(logit_c[:, :], bank[7][:, 0:NX]).then_inc(logit_c_done, 1)
                    if j == 1 and k >= 2:
                        ln_modulate(1, k - 2)
                    if j == 2 and k:
                        add_attention(k - 1)
                    if j == 4 and k:
                        dve.wait_ge(wo_ev, k)
                        ln_statistics(1, k - 1)
                    if j == 5 and 2 <= k < B:
                        choose(k - 2)
                    if j == 6 and k:
                        ln_normalise(1, k - 1)
                    if j == 6 and k == B:
                        choose(B - 2)
                    if j == 7 and 2 <= k < B:
                        weights_of(k - 2)
            ln_modulate(1, B - 1)

            def evacuate_gates(b):
                dve.wait_ge(gt_mm, b + 1)
                v.tensor_copy(gates_t[:, b * S:(b + 1) * S], bank[6][0:NX, :]).then_inc(gt_ev, 1)

            def start_sum(b):
                dve.wait_ge(b2_mm, b + 1)
                v.tensor_copy(acc[:, b * QT:(b + 1) * QT, :],
                              bank[7][:, :].rearrange("p (i e) -> p i e", i=QT)).then_inc(acc_set, 1)

            def hidden_split(e, tb):
                n = e * B + tb
                w = tb % 2
                if not (isinstance(n, int) and n < 2):
                    dve.wait_ge(down_mm, n - 1)
                for f in (2, 3, 0, 1):
                    if f < 2:
                        dve.wait_ge(g_hi_a, n * 2 + (f + 1))
                    else:
                        dve.wait_ge(gelu_done, n * FT + (f + 1))
                        v.tensor_copy(g_hi[w][f], g_f32[w][f]).then_inc(g_hi_v, 1)
                        dve.wait_ge(g_hi_v, n * 2 + (f - 1))
                    v.tensor_tensor(g_lo[w][f], g_f32[w][f], g_hi[w][f], ALU.subtract).then_inc(g_split, 1)

            def weigh_output(e, tb):
                n = e * B + tb
                dve.wait_ge(down_mm, n + 1)
                if not (isinstance(n, int) and n < 2):
                    dve.wait_ge(acc_add, n - 1)
                v.tensor_tensor(weighted[tb % 2].rearrange("p (i e) -> p i e", i=QT),
                                bank[4 + tb % 2][:, :].rearrange("p (i e) -> p i e", i=QT),
                                gates[:, tb * QT:(tb + 1) * QT, ds(e, 1)].broadcast_to([128, QT, E]),
                                ALU.mult).then_inc(weigh, 1)

            def expert(e):
                for tb in range(B):
                    n = e * B + tb if isinstance(e, int) else 2 * B
                    if 2 <= n < 2 + B:
                        evacuate_gates(n - 2)
                    hidden_split(e, tb)
                    if n == 0:
                        choose(B - 1)
                    if n == 1:
                        weights_of(B - 2)
                        weights_of(B - 1)
                    if tb:
                        weigh_output(e, tb - 1)
                    elif n:
                        weigh_output(e - 1, B - 1)
                    if 2 <= n < 2 + B:
                        start_sum(n - 2)

            expert(0)
            expert(1)
            with dve.Fori(2, NX) as e:
                expert(e)
            def finish(b):
                tiles = acc[:, b * QT:(b + 1) * QT, :]
                dve.wait_ge(acc_add, B * (NX - 1) + b + 1)
                step(v.tensor_tensor(tiles, tiles, gate_b[:, b, :].unsqueeze(1).broadcast_to([128, QT, E]), ALU.mult))
                v.tensor_tensor(tiles, tiles, x_tok[:, b * QT:(b + 1) * QT, :], ALU.add).then_inc(fin, 1)

            for b in range(B):
                if b == B - 2:
                    weigh_output(NX - 1, B - 1)
                finish(b)

        @block.gpsimd
        def _(pool):
            g = nc.gpsimd

            def rsqrt(ln, b):
                tiles = slice(b * QT, (b + 1) * QT)
                pool.wait_ge(consts, 5)
                pool.wait_ge(ln_var, ln * B + b + 1)
                g.tensor_tensor(rstd[:, tiles], var_e[:, tiles], half[:, tiles], ALU.pow).then_inc(ln_rstd, 1)

            def rotated(hp, b, m):
                n = (hp * B + b) * 2 + m
                if not (isinstance(n, int) and n < 2):
                    pool.wait_ge(rot_sum, n - 1)
                pool.wait_ge(raw_done, n + 1)
                g.tensor_tensor(rot_c[m][:, :], raw[m][:, :], rope[:, 0, :], ALU.mult).then_inc(cos_done, 1)
                pool.wait_ge(cos_done, n + 1)
                pool.wait_ge(sin_done, n + 1)
                if not (isinstance(n, int) and n < 2):
                    pool.wait_ge(qk_lo_done, n - 1)
                g.tensor_tensor(rot[m][:, :], rot_c[m][:, :], rot_s[m][:, :], ALU.add).then_inc(rot_sum, 1)
                pool.wait_ge(qk_hi_done, n + 1)
                g.tensor_tensor(qk_lo[m][b], rot[m][:, :], qk_hi[m][b], ALU.subtract).then_inc(qk_lo_done, 1)

            for b in range(B):
                rsqrt(0, b)
            pool.wait_ge(ld_b, 48)
            for b in range(B):
                for m in range(2):
                    rotated(0, b, m)
            with pool.Fori(1, HP) as hp:
                for b in range(B):
                    for m in range(2):
                        rotated(hp, b, m)

            def split_weights(e, w):
                pool.wait_ge(consts, 5)
                if not (isinstance(e, int) and e == 0):
                    pool.wait_ge(wx_split, e)
                pool.wait_ge(wx_ld[w], (e - w) * 16 + 32)
                g.tensor_tensor(wx_f32, wx_raw[w], ws_col[:, 0:1].broadcast_to([128, 2 * F]), ALU.mult).then_inc(wx_own, 1)
                pool.wait_ge(wx_own, e + 1)
                pool.wait_ge(wx_hi_done, e + 1)
                g.tensor_tensor(wx_lo[w], wx_f32, wx_hi[w], ALU.subtract).then_inc(wx_split, 1)

            def gather(e, tb):
                n = e * B + tb
                pool.wait_ge(weigh, n + 1)
                part = acc[:, tb * QT:(tb + 1) * QT, :]
                g.tensor_tensor(part, part, weighted[tb % 2].rearrange("p (i e) -> p i e", i=QT), ALU.add).then_inc(acc_add, 1)

            def tokens_low(b):
                pool.wait_ge(ln_hi, B + b + 1)
                toks = slice(b * S, (b + 1) * S)
                g.tensor_tensor(h_lo[:, toks], h_f32[:, toks], h_hi[:, toks], ALU.subtract).then_inc(ln_lo, 1)

            split_weights(0, 0)
            for b in range(B):
                if b < B - 1:
                    pool.wait_ge(o_biased, b + 1)
                    mid = o_mid[b % 2][:, :].rearrange("p (i e) -> p i e", i=QT)
                    tiles = x_tok[:, b * QT:(b + 1) * QT, :]
                    g.tensor_tensor(mid, mid, gate_a[:, b, :].unsqueeze(1).broadcast_to([128, QT, E]), ALU.mult).then_inc(o_gated, 1)
                    pool.wait_ge(o_gated, b + 1)
                    g.tensor_tensor(tiles, tiles, mid, ALU.add).then_inc(wo_ev, 1)
                if b:
                    tokens_low(b - 1)
                rsqrt(1, b)
            tokens_low(B - 1)
            split_weights(1, 1)
            for tb in range(B):
                pool.wait_ge(acc_set, tb + 1)
                gather(0, tb)
            with pool.Fori(1, NX // 2) as pair:
                for w in range(2):
                    split_weights(pair * 2 + w, w)
                    for tb in range(B):
                        gather(pair * 2 + w - 1, tb)
            for tb in range(B):
                gather(NX - 1, tb)


_OUTS = [((TOK, E), 'float32')]


def kernel(**inputs):
    import numpy as np
    import concourse.bacc as bacc
    from concourse.bass_utils import run_bass_kernel_spmd

    def arr(name):
        return np.asarray(inputs[name])

    wq, wk, wv = arr("L0_attn_wq"), arr("L0_attn_wk"), arr("L0_attn_wv")
    bq, bk = arr("L0_attn_bq"), arr("L0_attn_bk")
    laid = {
        "x": arr("L0_attn_x").reshape(TOK, E),
        "c_t": arr("L0_c").T,
        "wmod": arr("L0_wmod"),
        "w_qkv": np.concatenate([w.T for w in (wq, wk, wv)], axis=1),
        "b_qk": np.stack([v.reshape(HP, 128).T for v in (bq, bk)], axis=1),
        "bv_t": arr("L0_attn_bv").reshape(HP, 128).T,
        "wo_t": arr("L0_attn_wo").T.reshape(HP, 128, E).transpose(1, 0, 2).reshape(128, HP * E),
        "bo_rows": np.broadcast_to(arr("L0_attn_bo"), (128, E)),
        "keys_t": arr("L0_ffn_keys").T,
        "rw_t": arr("L0_ffn_rw").T,
        "rb_row": arr("L0_ffn_rb").reshape(1, NX),
        "w1_t": arr("L0_ffn_w1").transpose(0, 2, 1),
        "b1_t": arr("L0_ffn_b1").reshape(NX, FT, 128).transpose(2, 0, 1),
        "w2_t": arr("L0_ffn_w2").transpose(0, 2, 1).reshape(NX, FT, 128, E).transpose(0, 2, 1, 3).reshape(NX, 128, FT * E),
        "b2": arr("L0_ffn_b2"),
    }
    theta = np.float64(10000.0) ** (np.arange(0, DH, 2) / DH)
    freqs = np.arange(S, dtype=np.float32)[:, None] * (np.float32(1.0) / theta.astype(np.float32))[None, :]
    angle = np.concatenate([freqs, freqs], axis=1).astype(np.float64).T
    sign = np.where(np.arange(DH) % 2 == 0, -1.0, 1.0)[:, None]
    table = np.stack([np.cos(angle), np.sin(angle) * sign], axis=1)
    laid["cos_sin"] = np.concatenate([table, table], axis=0).astype(np.float32)
    query, key = np.arange(128)[:, None], np.arange(128)[None, :]
    laid["causal"] = np.concatenate([np.zeros((128, S - 128)), np.where(key > query, NEG, 0.0)], axis=1).astype(np.float32)
    laid["identity"] = np.eye(128, dtype=np.float32)

    nc = bacc.Bacc("TRN2", target_bir_lowering=False, num_devices=1)
    arrays, aps = {}, {}
    for name, a in laid.items():
        a = np.ascontiguousarray(a)
        arrays[f"in_{name}"] = a
        aps[name] = nc.dram_tensor(f"in_{name}", a.shape, mybir.dt.from_np(a.dtype), kind="ExternalInput").ap()
    out = nc.dram_tensor("out_0", (TOK, E), mybir.dt.float32, kind="ExternalOutput").ap()
    adaln_block(nc, out=out, **aps)
    got = run_bass_kernel_spmd(nc, [arrays], core_ids=[0])
    return got.results[0]["out_0"].reshape(B, S, E)
```
